# Optimizing a Trainium2 kernel written in Bass

```python
import numpy as np
import jax
import jax.numpy as jnp

def _softmax(x, axis=-1):
    return jax.nn.softmax(x, axis=axis)

def _gelu(x):
    return jax.nn.gelu(x, approximate=True)

def _silu(x):
    return jax.nn.silu(x)

def _sigmoid(x):
    return jax.nn.sigmoid(x)

def _layernorm(x, axis=-1, eps=1e-05):
    m = jnp.mean(x, axis=axis, keepdims=True)
    v = jnp.var(x, axis=axis, keepdims=True)
    return (x - m) / jnp.sqrt(v + eps)

def _scatter_add(tgt, idx, src, axis=0):
    return tgt.at[idx].add(src)

def _segment_sum(src, seg, n):
    return jax.ops.segment_sum(src, seg, n)
kernel_name = 'mk_flamingo_gated_d1_seqx_r4_7540d6'

def setup_inputs(seed: int=0):
    np.random.seed(seed)
    _w = jnp.asarray

    def _rec_inputs():
        import jax
        import jax.numpy as jnp
        _rk = jax.random.key(seed)
        x = 7.22e-05 + 1 * jax.random.normal(jax.random.fold_in(_rk, 1), (64, 128, 512), jnp.float32)
        _lenS = 128 - jax.random.randint(jax.random.fold_in(_rk, 7), (64,), 0, max(1, 128 // 4) + 1, jnp.int32)
        _lenS2 = 128 - jax.random.randint(jax.random.fold_in(_rk, 8), (64,), 0, max(1, 128 // 4) + 1, jnp.int32)
        _ctx_512P = jax.random.normal(jax.random.fold_in(_rk, 11), (64, 16, 128), jnp.float32)
        _ctx_512c = jax.random.dirichlet(jax.random.fold_in(_rk, 511), 0.3 * jnp.ones((16,), jnp.float32), (64, 128))
        _ctx_512t = jnp.einsum('bsk,bkd->bsd', _ctx_512c, _ctx_512P)
        _ctx_512t = _ctx_512t * jax.lax.rsqrt(jnp.mean(jnp.square(_ctx_512t)) + 1e-12) * 0.953939
        ctx_512 = -0.000514642 + 1.00011 * (_ctx_512t + 0.3 * jax.random.normal(jax.random.fold_in(_rk, 611), (64, 128, 128), jnp.float32))
        _g = jax.random.normal(jax.random.fold_in(_rk, 9001), (2, 1), jnp.float32)
        _g = jnp.sign(_g) * jnp.maximum(jnp.abs(_g), 1.0) + (_g == 0) * 1.0
        g_xattn = _g[0]
        g_ffn = _g[1]
        return (x, ctx_512, g_xattn, g_ffn)
    x, ctx_512, g_xattn, g_ffn = _rec_inputs()

    def _L0_xattn_setup():
        import jax, jax.numpy as jnp
        import numpy as np
        import math
        NUM_Q_HEADS = 32
        NUM_KV_HEADS = 8
        key = jax.random.key(seed)
        k1, k2, k3 = jax.random.split(key, 3)
        B, S, E = (2, 512, 512)
        kv_E = NUM_KV_HEADS * (E // NUM_Q_HEADS)
        q = jax.random.normal(k1, (B, S, E), dtype=jnp.float32)
        k = jax.random.normal(k2, (B, S, kv_E), dtype=jnp.float32)
        v = jax.random.normal(k3, (B, S, kv_E), dtype=jnp.float32)
        return {'q': q, 'k': k, 'v': v}
    _L0_xattn_all = _L0_xattn_setup()
    _L0_xattn_in = {k: v for k, v in _L0_xattn_all.items() if k in ()}
    del _L0_xattn_all

    def _L0_ffn_setup():
        import jax, jax.numpy as jnp
        import numpy as np
        B, S, H = (1, 256, 512)
        E, K = (32, 4)
        F, FS = (352, 1408)
        CAP = 64

        def silu(x):
            return x * jax.nn.sigmoid(x)
        key = jax.random.key(seed)
        ks = jax.random.split(key, 9)
        sc = 0.02
        return {'hidden_states': jax.random.normal(ks[0], (B, S, H), jnp.float32), 'Wr': jax.random.normal(ks[1], (H, E), jnp.float32) * sc, 'Wg': jax.random.normal(ks[2], (E, H, F), jnp.float32) * sc, 'Wu': jax.random.normal(ks[3], (E, H, F), jnp.float32) * sc, 'Wd': jax.random.normal(ks[4], (E, F, H), jnp.float32) * sc, 'Wsg': jax.random.normal(ks[5], (H, FS), jnp.float32) * sc, 'Wsu': jax.random.normal(ks[6], (H, FS), jnp.float32) * sc, 'Wsd': jax.random.normal(ks[7], (FS, H), jnp.float32) * sc, 'Wse': jax.random.normal(ks[8], (H, 1), jnp.float32) * sc}
    _L0_ffn_all = _L0_ffn_setup()
    _L0_ffn_in = {k: v for k, v in _L0_ffn_all.items() if k in ('Wr', 'Wg', 'Wu', 'Wd', 'Wsg', 'Wsu', 'Wsd', 'Wse')}
    del _L0_ffn_all
    return {'x': x, 'ctx_512': ctx_512, 'g_xattn': g_xattn, 'g_ffn': g_ffn, 'L0_ffn_Wr': _L0_ffn_in['Wr'], 'L0_ffn_Wg': _L0_ffn_in['Wg'], 'L0_ffn_Wu': _L0_ffn_in['Wu'], 'L0_ffn_Wd': _L0_ffn_in['Wd'], 'L0_ffn_Wsg': _L0_ffn_in['Wsg'], 'L0_ffn_Wsu': _L0_ffn_in['Wsu'], 'L0_ffn_Wsd': _L0_ffn_in['Wsd'], 'L0_ffn_Wse': _L0_ffn_in['Wse']}

def reference(x, ctx_512, g_xattn, g_ffn, L0_ffn_Wr, L0_ffn_Wg, L0_ffn_Wu, L0_ffn_Wd, L0_ffn_Wsg, L0_ffn_Wsu, L0_ffn_Wsd, L0_ffn_Wse):
    import jax
    import jax.numpy as jnp

    def _L0_xattn_ref(q, k, v):
        import jax, jax.numpy as jnp
        import numpy as np
        import math
        NUM_Q_HEADS = 32
        NUM_KV_HEADS = 8
        B, S, E = q.shape
        H, KV = (NUM_Q_HEADS, NUM_KV_HEADS)
        D = E // H
        G = H // KV
        scale = math.sqrt(D)
        qh = q.reshape(B, S, KV, G, D).transpose(0, 2, 3, 1, 4)
        kh = k.reshape(B, S, KV, D).transpose(0, 2, 1, 3)
        vh = v.reshape(B, S, KV, D).transpose(0, 2, 1, 3)
        scores = jnp.einsum('bkgsd,bktd->bkgst', qh, kh) / scale
        weights = jax.nn.softmax(scores, axis=-1)
        out = jnp.einsum('bkgst,bktd->bkgsd', weights, vh)
        return out.transpose(0, 3, 1, 2, 4).reshape(B, S, E)

    def _L0_ffn_ref(hidden_states, Wr, Wg, Wu, Wd, Wsg, Wsu, Wsd, Wse):
        import jax, jax.numpy as jnp
        import numpy as np
        B, S, H = (1, 256, 512)
        E, K = (32, 4)
        F, FS = (352, 1408)
        CAP = 64

        def silu(x):
            return x * jax.nn.sigmoid(x)
        b, s_len, h = hidden_states.shape
        x = hidden_states.reshape(-1, h)
        T = x.shape[0]
        probs = jax.nn.softmax(x @ Wr, axis=-1)
        topw, topi = jax.lax.top_k(probs, K)
        topw = topw / jnp.sum(topw, axis=-1, keepdims=True)
        shared = silu(x @ Wsg) * (x @ Wsu) @ Wsd
        shared = shared * jax.nn.sigmoid(x @ Wse)
        sel = topi.reshape(-1)
        w = topw.reshape(-1)
        tok = jnp.repeat(jnp.arange(T), K)
        oh = jax.nn.one_hot(sel, E, dtype=jnp.int32)
        pos = (jnp.cumsum(oh, axis=0) * oh).sum(-1) - 1
        valid = (pos < CAP).astype(x.dtype)
        posc = jnp.clip(pos, 0, CAP - 1)
        xe = jnp.zeros((E, CAP, h), x.dtype).at[sel, posc].add(x[tok] * valid[:, None])
        g = silu(jnp.einsum('ech,ehf->ecf', xe, Wg))
        u = jnp.einsum('ech,ehf->ecf', xe, Wu)
        ye = jnp.einsum('ecf,efh->ech', g * u, Wd)
        y_pair = ye[sel, posc] * (w * valid)[:, None]
        out = shared.at[tok].add(y_pair)
        return out.reshape(b, s_len, h)
    x = x + jnp.tanh(g_xattn[0]) * _L0_xattn_ref(_layernorm(x, axis=-1), ctx_512, ctx_512)
    x = x + jnp.tanh(g_ffn[0]) * _L0_ffn_ref(_layernorm(x, axis=-1), L0_ffn_Wr, L0_ffn_Wg, L0_ffn_Wu, L0_ffn_Wd, L0_ffn_Wsg, L0_ffn_Wsu, L0_ffn_Wsd, L0_ffn_Wse)
    return x

_drawn_inputs = setup_inputs


def setup_inputs(seed=0):
    import zlib

    import numpy as np

    out = dict(_drawn_inputs(seed))
    spreads = {}
    factors = {'L0_ffn_Wr': 8.0,
     'L0_ffn_Wg': 8.0,
     'L0_ffn_Wu': 8.0,
     'L0_ffn_Wd': 8.0,
     'L0_ffn_Wse': 64.0,
     'L0_ffn_Wsg': 5.636,
     'L0_ffn_Wsu': 5.511,
     'L0_ffn_Wsd': 5.522}
    for name, (base, spread) in spreads.items():
        noise = np.random.default_rng([zlib.crc32(name.encode()), seed]).standard_normal(out[name].shape)
        drawn = base * np.exp(spread * noise) if base else spread * noise
        out[name] = jnp.asarray(drawn.astype(out[name].dtype))
    for name, factor in factors.items():
        out[name] = (out[name] * factor).astype(out[name].dtype)
    return out
```

```python
import concourse.bass as bass
from concourse import mybir
from contextlib import ExitStack

F32 = mybir.dt.float32
F32R = mybir.dt.float32r
U32 = mybir.dt.uint32
I32 = mybir.dt.int32
ALU = mybir.AluOpType
ACT = mybir.ActivationFunctionType
AX = mybir.AxisListType

NB, S, E = 64, 128, 512
NH, NKV, D = 32, 8, 16
G = NH // NKV
KC = E // 128
TOK = NB * S
NE, TOPK, CAP = 32, 4, 64
FE, FS = 352, 1408
FC = FS // 128
EPS = 1e-5
NC = 4
TILE = 512
NT = TOK // TILE
TB = TILE // S
NPAIR = NE // 2
FEC = [(0, 128), (128, 128), (256, FE - 256)]


def wait(eng, sem, value):
    if not isinstance(value, int) or value > 0:
        eng.wait_ge(sem, value)


def alone(eng, sem):
    eng.sem_inc(sem, 1)


class Count:

    def __init__(self, sem):
        self.sem, self.at, self.base, self.turn = sem, 0, 0, 0

    def inc(self, ins, n=1):
        self.at += n
        ins.then_inc(self.sem, n)

    def value(self):
        return self.base + self.at + self.turn

    def wait(self, eng):
        eng.wait_ge(self.sem, self.value())


class Batch:

    def __init__(self, pair, off):
        self.pair, self.off = pair, off

    def __add__(self, n):
        return Batch(self.pair, self.off + n)

    def __sub__(self, n):
        return Batch(self.pair, self.off - n)

    @property
    def n(self):
        return 2 * self.pair + self.off

    @property
    def half(self):
        return self.pair + self.off // 2

    @property
    def par(self):
        return self.off % 2

    @property
    def ok(self):
        return not isinstance(self.pair, int) or 0 <= self.n < NB


def build(nc, x, ctx_in, g_xattn, g_ffn, Wr, Wg, Wu, Wd, Wsg, Wsu, Wsd, Wse, out):
    x_t = x
    out_rows = out.rearrange("b s e -> (b s) e")
    xn_dram = nc.dram_tensor("xn_rows", (TOK, E), F32, kind="Internal").ap()
    xT_dram = nc.dram_tensor("xn_cols", (KC, 128, TOK), F32, kind="Internal").ap()
    rw_dram = nc.dram_tensor("route_rows", (TOK, 2 * TOPK), F32, kind="Internal").ap()

    stack = ExitStack()
    with stack:
        def maker(scope):
            def sb(name, shape, dt=F32):
                return scope.enter_context(nc.sbuf_tensor(name, shape, dt))

            def ps(name, shape, dt=F32):
                return scope.enter_context(nc.psum_tensor(name, shape, dt))

            def sem(name):
                return scope.enter_context(nc.semaphore(name))
            return sb, ps, sem

        sb, _, sem = maker(stack)
        ident = sb("ident", [128, 128])
        tanh_x = sb("tanh_x", [128, 1])
        tanh_f = sb("tanh_f", [128, 1])
        slot_idx = sb("slot_idx", [128, NPAIR], U32)
        half_idx = sb("half_idx", [CAP, 2, NPAIR], U32)
        half_tok = sb("half_tok", [CAP, 2, NPAIR], U32)
        half_used = sb("half_used", [CAP, 2, NPAIR])
        gate_s = sb("gate_s", [128, NB])
        routing = stack.enter_context(ExitStack())
        sb, _, _ = maker(routing)
        top_val = sb("top_val", [128, NB * TOPK])
        top_idx = sb("top_idx", [128, NB * TOPK])
        gate_z = sb("gate_z", [128, NB])
        chosen = sb("chosen", [128, NB, NE])

        with ExitStack() as scope:
            sb, ps, sem = maker(scope)
            xs = [sb(f"xs{i}", [128, E]) for i in range(2)]
            xres = [sb(f"xres{i}", [128, E]) for i in range(2)]
            kv = [sb(f"kv{i}", [128, NKV * D]) for i in range(2)]
            vals = [sb(f"vals{i}", [128, NKV, 32]) for i in range(2)]
            ks = sb("ks", [128, NKV, 64])
            qraw = sb("qraw", [128, E])
            qs = [sb(f"qs{i}", [128, NC, G, 2, 64]) for i in range(2)]
            qt = [sb(f"qt{i}", [128, NC, G * 128], F32R) for i in range(2)]
            kt = [sb(f"kt{i}", [128, NC, 2 * 128], F32R) for i in range(2)]
            probs = [sb(f"probs{i}", [128, 2 * 512]) for i in range(4)]
            ot_sb = [sb(f"ot_sb{i}", [128, 512]) for i in range(2)]
            o_sb = sb("o_sb", [128, E])
            rec = sb("rec", [128, 16])
            x2 = [sb(f"x2_{i}", [128, E]) for i in range(2)]
            xn = [sb(f"xn_{i}", [128, E]) for i in range(2)]
            xnT = [sb(f"xnT{i}", [128, KC, 128]) for i in range(2)]
            wr = sb("wr", [128, KC, NE + 1])
            negmax = [sb(f"negmax{i}", [128, 8]) for i in range(2)]
            mt = [sb(f"mt{i}", [8, 128], F32R) for i in range(2)]
            st1, st2 = sb("st1", [128, 6]), sb("st2", [128, 6])
            mv1 = [sb(f"mv1_{i}", [128, 2]) for i in range(2)]
            mv2 = [sb(f"mv2_{i}", [128, 2]) for i in range(2)]
            ve1, rs1 = sb("ve1", [128, 1]), sb("rs1", [128, 1])
            ve2, rs2 = sb("ve2", [128, 1]), sb("rs2", [128, 1])
            mhalf = sb("mhalf", [128, 1])
            lg = sb("lg", [128, NE + 1])
            v8 = sb("v8", [128, 8])
            i8 = sb("i8", [128, 8], U32)
            idxf = sb("idxf", [128, TOPK])
            eqs = sb("eqs", [128, TOPK, NE])
            iota_e = sb("iota_e", [128, NE])
            gx, gf = sb("gx", [128, 1]), sb("gf", [128, 1])

            p_max = ps("p_max", [128, 2, 512])
            p_exp = ps("p_exp", [128, 2, 512])
            p_tq = ps("p_tq", [128, 512])
            p_pv = ps("p_pv", [128, 512])
            p_ot = ps("p_ot", [128, 512])
            p_ms = ps("p_ms", [128, 512])

            x_in = [sem(f"x_in{i}") for i in range(2)]
            kv_in = [sem(f"kv_in{i}") for i in range(2)]
            xres_in = [sem(f"xres_in{i}") for i in range(2)]
            v_in = [sem(f"v_in{i}") for i in range(2)]
            mrow_in = [sem(f"mrow_in{i}") for i in range(2)]
            x2_out = [sem(f"x2_out{i}") for i in range(2)]
            xn_out = [sem(f"xn_out{i}") for i in range(2)]
            xnT_out = [sem(f"xnT_out{i}") for i in range(2)]
            wr_in, g_in = sem("wr_in"), sem("g_in")
            spare_d, spare_p, spare_s = sem("spare_d"), sem("spare_p"), sem("spare_s")
            consts, tanh_done = sem("consts"), sem("tanh_done")
            pads, id0 = sem("pads"), sem("id0")
            stat1, stat2 = sem("stat1"), sem("stat2")
            ks_done, qs_done, xn_done = sem("ks_done"), sem("qs_done"), sem("xn_done")
            pool_chain, dve_chain = sem("pool_chain"), sem("dve_chain")
            tq_mm, k_mm, p1_mm, p2_mm = sem("tq_mm"), sem("k_mm"), sem("p1_mm"), sem("p2_mm")
            pv_mm, ot_mm, mt_mm = sem("pv_mm"), sem("ot_mm"), sem("mt_mm")
            xnT_mm, lg_mm = sem("xnT_mm"), sem("lg_mm")
            max_done, exp_done, tq_done = sem("max_done"), sem("exp_done"), sem("tq_done")
            kt_done, pv_done, mt_done = sem("kt_done"), sem("pv_done"), sem("mt_done")
            ot_done, x2_done, xnT_done, lg_done = sem("ot_done"), sem("x2_done"), sem("xnT_done"), sem("lg_done")

            FIRST, LAST = 5, 61

            def iterations(eng, body, count=None):
                for b in range(FIRST):
                    body(Batch((b - 1) // 2, b - 2 * ((b - 1) // 2)))
                start = count.at if count else 0
                with eng.Fori((FIRST - 1) // 2, (LAST - 1) // 2) as pair:
                    if count:
                        count.turn = (pair - (FIRST - 1) // 2) * count.per_turn
                    body(Batch(pair, 1))
                    body(Batch(pair, 2))
                if count:
                    assert count.at - start == count.per_turn, count.at - start
                    count.turn = 0
                    count.at = start + count.per_turn * ((LAST - FIRST) // 2)
                for b in range(LAST, NB + 3):
                    body(Batch((b - 1) // 2, b - 2 * ((b - 1) // 2)))

            block = scope.enter_context(nc.Block())

            @block.sync
            def _(sp):
                sp.dma_start(wr[:, :, 0:NE], Wr.rearrange("(k p) e -> p k e", p=128)).then_inc(wr_in, 16)
                sp.dma_start(wr[:, :, NE:NE + 1], Wse.rearrange("(k p) e -> p k e", p=128),
                             allow_slow_non_contiguous=True).then_inc(wr_in, 16)
                sp.dma_start(gx[:, :], g_xattn.rearrange("(a n) -> a n", a=1).to_broadcast([128, 1])).then_inc(g_in, 16)
                sp.dma_start(gf[:, :], g_ffn.rearrange("(a n) -> a n", a=1).to_broadcast([128, 1])).then_inc(g_in, 16)

                def load_in(b):
                    wait(sp, qs_done, b.n - 1)
                    sp.dma_start(xs[b.par][:, :], x_t[b.n]).then_inc(x_in[b.par], 16)
                    sp.dma_start(kv[b.par][:, :], ctx_in[b.n]).then_inc(kv_in[b.par], 16)

                def body(B):
                    if isinstance(B.n, int) and B.n == 0:
                        load_in(B)
                        load_in(B + 1)
                    for c in range(NC):
                        m = (B - 1, 3) if c == 0 else (B, c - 1)
                        if m[0].ok:
                            b, cc = m
                            wait(sp, mt_done, 4 * b.n + cc + 1)
                            for g2 in range(2):
                                sp.dma_start(qt[b.par][64 * g2:64 * g2 + 1, cc, :].bitcast(F32),
                                             mt[cc % 2][4 * g2:4 * g2 + 4, :].bitcast(F32)).then_inc(mrow_in[cc % 2], 16)
                        if c == 0:
                            if (B + 2).ok:
                                load_in(B + 2)
                            if (B - 1).ok:
                                wait(sp, x2_done, (B - 1).n - 1)
                                sp.dma_start(xres[(B - 1).par][:, :], x_t[(B - 1).n]).then_inc(xres_in[(B - 1).par], 16)
                            if (B - 3).ok:
                                b = B - 3
                                wait(sp, xn_done, b.n + 1)
                                sp.dma_start(xn_dram[bass.ts(b.n, 128), :], xn[b.par][:, :]).then_inc(xn_out[b.par], 16)
                        if c == 1:
                            if B.ok:
                                wait(sp, pv_mm, 2 * (B.n - 1))
                                if isinstance(B.n, int) and B.n < 2:
                                    sp.wait_ge(pads, 4)
                                sp.dma_start(vals[B.par][:, :, 0:D], ctx_in[B.n].rearrange("t (g d) -> t g d", d=D)).then_inc(v_in[B.par], 16)
                            if (B - 3).ok:
                                b = B - 3
                                wait(sp, xnT_done, b.n + 1)
                                alone(sp, spare_s)
                                sp.dma_start(xT_dram[:, :, bass.ts(b.n, 128)].rearrange("k p t -> p k t"), xnT[b.par][:, :, :]).then_inc(xnT_out[b.par], 16)
                        if c == 2 and (B - 2).ok:
                            b = B - 2
                            wait(sp, x2_done, b.n + 1)
                            sp.dma_start(out_rows[bass.ts(b.n, 128), :], x2[b.par][:, :]).then_inc(x2_out[b.par], 16)
                iterations(sp, body)
                for s in (x2_out, xn_out, xnT_out):
                    for i in range(2):
                        sp.wait_ge(s[i], 16 * (NB // 2))

            @block.gpsimd
            def _(pool):
                nc.gpsimd.memset(ident[:, :], 0.0).then_inc(id0, 1)
                pool.wait_ge(id0, 1)
                nc.gpsimd.affine_select(out=ident[:, :], in_=ident[:, :], compare_op=ALU.not_equal, fill=1.0, base=0,
                                        pattern=[[-1, 128]], channel_multiplier=1).then_inc(consts, 1)
                nc.gpsimd.iota(iota_e[:, :], pattern=[[1, NE]], base=0, channel_multiplier=0,
                               allow_small_or_imprecise_dtypes=True).then_inc(consts, 1)
                nc.gpsimd.memset(mhalf[:, :], -0.5).then_inc(id0, 1)
                pool.wait_ge(id0, 2)
                pool.wait_ge(pads, 8)
                chain = Count(pool_chain)

                def body(B):
                    b = B + 1
                    if B.ok and isinstance(B.n, int) and B.n == 0:
                        prepare(B, chain)
                    if b.ok:
                        prepare(b, chain)
                    b = B - 2
                    if b.ok:
                        pool.wait_ge(stat2, b.n + 1)
                        alone(pool, spare_p)
                        chain.inc(nc.gpsimd.tensor_scalar(ve2[:, :], mv2[b.par][:, 1:2], EPS, None, ALU.add))
                        chain.wait(pool)
                        chain.inc(nc.gpsimd.tensor_tensor(rs2[:, :], ve2[:, :], mhalf[:, :], ALU.pow))
                        chain.wait(pool)
                        wait(pool, xnT_mm, b.n - 1)
                        wait(pool, xn_out[b.par], 16 * b.half)
                        alone(pool, spare_p)
                        nc.gpsimd.tensor_scalar(xn[b.par][:, :], x2[b.par][:, :], mv2[b.par][:, 0:1], rs2[:, 0:1],
                                                ALU.subtract, ALU.mult).then_inc(xn_done, 1)

                def prepare(b, chain):
                    pool.wait_ge(kv_in[b.par], 16 * (b.half + 1))
                    wait(pool, k_mm, b.n)
                    alone(pool, spare_p)
                    kin = kv[b.par][:, :].rearrange("p (g d) -> p g d", d=D)
                    nc.gpsimd.tensor_scalar(ks[:, :, 16:32].bitcast(F32R), kin, 1.0, None, ALU.mult)
                    chain.inc(nc.gpsimd.tensor_scalar(ks[:, :, 48:64].bitcast(F32R), kin, 1.0, None, ALU.mult))
                    chain.wait(pool)
                    nc.gpsimd.tensor_tensor(ks[:, :, 32:48], kin, ks[:, :, 16:32], ALU.subtract).then_inc(ks_done, 1)
                    pool.wait_ge(stat1, b.n + 1)
                    alone(pool, spare_p)
                    chain.inc(nc.gpsimd.tensor_scalar(ve1[:, :], mv1[b.par][:, 1:2], EPS, None, ALU.add))
                    chain.wait(pool)
                    chain.inc(nc.gpsimd.tensor_tensor(rs1[:, :], ve1[:, :], mhalf[:, :], ALU.pow))
                    chain.wait(pool)
                    pool.wait_ge(x_in[b.par], 16 * (b.half + 1))
                    wait(pool, tq_mm, 4 * (b.n - 1))
                    alone(pool, spare_p)
                    m, r = mv1[b.par][:, 0:1], rs1[:, 0:1]
                    def stack(part, g2):
                        return qs[b.par][:, :, :, g2, 16 * part:16 * part + 16]

                    def heads(t, g2):
                        return t.rearrange("p (c g i d) -> p c g i d", g=2, i=G, d=D)[:, :, g2, :, :]

                    nc.gpsimd.tensor_scalar(qraw[:, :], xs[b.par][:, :], m, r, ALU.subtract, ALU.mult)
                    for part in (1, 2):
                        for g2 in range(2):
                            last = nc.gpsimd.tensor_scalar(stack(part, g2).bitcast(F32R), heads(xs[b.par][:, :], g2), m, r,
                                                           ALU.subtract, ALU.mult)
                    chain.inc(last)
                    chain.wait(pool)
                    for g2 in range(2):
                        last = nc.gpsimd.tensor_tensor(stack(3, g2), heads(qraw[:, :], g2), stack(1, g2), ALU.subtract)
                    last.then_inc(qs_done, 1)
                chain.per_turn = 2 * (4 + 2)
                iterations(pool, body, chain)

            @block.scalar
            def _(act):
                act.wait_ge(g_in, 32)
                nc.scalar.activation(tanh_x[:, :], gx[:, :], ACT.Tanh).then_inc(tanh_done, 1)
                nc.scalar.activation(tanh_f[:, :], gf[:, :], ACT.Tanh).then_inc(tanh_done, 1)
                act.wait_ge(pads, 8)

                def k_evac(b):
                    act.wait_ge(k_mm, b.n + 1)
                    wait(act, p2_mm, 4 * (b.n - 1))
                    nc.scalar.activation(kt[b.par][0:64, :, 0:128], p_ms[0:64, :].rearrange("p (c t) -> p c t", c=NC), ACT.Copy)
                    nc.scalar.activation(kt[b.par][64:128, :, 128:256], p_ms[64:128, :].rearrange("p (c t) -> p c t", c=NC),
                                         ACT.Copy).then_inc(kt_done, 1)

                def q_evac(b, c):
                    act.wait_ge(tq_mm, 4 * b.n + c + 1)
                    wait(act, p2_mm, 4 * (b.n - 2) + c + 1)
                    nc.scalar.activation(qt[b.par][:, c, :], p_tq[:, :], ACT.Copy).then_inc(tq_done, 1)

                def pv_evac(b, s):
                    act.wait_ge(pv_mm, 2 * b.n + s + 1)
                    wait(act, ot_mm, 2 * (b.n - 1) + s + 1)
                    nc.scalar.activation(ot_sb[s][:, :], p_pv[:, :], ACT.Copy).then_inc(pv_done, 1)

                def body(B):
                    if isinstance(B.n, int) and B.n == 0:
                        k_evac(B)
                        q_evac(B, 0)
                    for c in range(NC):
                        b = B - 1
                        if b.ok:
                            act.wait_ge(p2_mm, 4 * b.n + c + 1)
                            wait(act, pv_mm, 2 * (b.n - 1) + c // 2 + 1)
                            nc.scalar.activation(probs[c][:, :], p_exp[:, :, :].rearrange("p a b -> p (a b)"), ACT.Exp,
                                                 scale=float(D) ** -0.5).then_inc(exp_done, 1)
                        if c == 0 and (B - 2).ok:
                            pv_evac(B - 2, 1)
                        if c == 2 and (B - 1).ok:
                            pv_evac(B - 1, 0)
                        b, cc = (B - 1, 3) if c == 0 else (B, c - 1)
                        if b.ok:
                            act.wait_ge(mt_mm, 4 * b.n + cc + 1)
                            wait(act, mrow_in[cc % 2], 32 * (2 * b.n + cc // 2))
                            nc.scalar.activation(mt[cc % 2][:, :], p_ms[0:8, 0:128], ACT.Copy).then_inc(mt_done, 1)
                        if c == 3 and (B + 1).ok:
                            k_evac(B + 1)
                        if c < 3 and B.ok:
                            q_evac(B, c + 1)
                        if c == 3 and (B + 1).ok:
                            q_evac(B + 1, 0)
                iterations(act, body)

            @block.vector
            def _(dve):
                for i in range(2):
                    nc.vector.memset(vals[i][:, :, 16:32], 0.0).then_inc(pads, 1)
                dve.wait_ge(pads, 2)
                for i in range(2):
                    nc.vector.memset(vals[i][:, :, 16:17], 1.0).then_inc(pads, 1)
                for i in range(2):
                    nc.vector.memset(qs[i][:, :, :, :, 0:16], 0.0).then_inc(pads, 1)
                nc.vector.memset(kt[0][:, :, :].bitcast(F32), 0.0)
                nc.vector.memset(kt[1][:, :, :].bitcast(F32), 0.0).then_inc(pads, 1)
                nc.vector.memset(ks[:, :, 0:16], 0.0).then_inc(dve_chain, 1)
                chain = Count(dve_chain)
                chain.at = 1
                chain.wait(dve)
                nc.vector.memset(ks[:, :, 0:1], 1.0).then_inc(pads, 1)
                dve.wait_ge(consts, 2)
                dve.wait_ge(tanh_done, 2)

                def stats(b, source, st, mv, done):
                    chain.inc(nc.vector.bn_stats(st[:, :], source))
                    chain.wait(dve)
                    alone(dve, spare_d)
                    nc.vector.bn_aggr(mv[b.par][:, :], st[:, :]).then_inc(done, 1)

                def stats_x(b):
                    dve.wait_ge(x_in[b.par], 16 * (b.half + 1))
                    wait(dve, qs_done, b.n - 1)
                    stats(b, xs[b.par][:, :], st1, mv1, stat1)

                def normalise(b, s):
                    dve.wait_ge(ot_mm, 2 * b.n + s + 1)
                    v = p_ot[:, :].rearrange("p (i q r) -> p i q r", i=G, q=4)
                    chain.inc(nc.vector.reciprocal(rec[:, :].rearrange("p (i q) -> p i q", i=G), v[:, :, :, D]))
                    chain.wait(dve)
                    if s == 0:
                        wait(dve, x2_done, b.n)
                    ov = o_sb[:, 256 * s:256 * s + 256].rearrange("p (q i d) -> p i q d", q=4, i=G)
                    rv = rec[:, :].rearrange("p (i q) -> p i q", i=G).unsqueeze(3).to_broadcast([128, G, 4, D])
                    nc.vector.tensor_tensor(ov, v[:, :, :, 0:D], rv, ALU.mult).then_inc(ot_done, 1)

                def body(B):
                    if isinstance(B.n, int) and B.n == 0:
                        stats_x(B)
                    for c in range(NC):
                        if B.ok:
                            dve.wait_ge(p1_mm, 4 * B.n + c + 1)
                            wait(dve, mt_mm, 4 * B.n + c - 1)
                            nc.vector.tensor_reduce(negmax[c % 2][:, :].rearrange("p (g i) -> p i g", i=G),
                                                    p_max[:, :, :].rearrange("p a (h g t) -> p (a h) g t", g=2, t=128),
                                                    AX.X, ALU.max, negate=True).then_inc(max_done, 1)
                        if c == 0:
                            if (B + 1).ok:
                                stats_x(B + 1)
                            if (B - 3).ok:
                                b = B - 3
                                dve.wait_ge(xnT_mm, b.n + 1)
                                wait(dve, xnT_out[b.par], 16 * b.half)
                                wait(dve, lg_mm, b.n - 1)
                                nc.vector.tensor_copy(xnT[b.par][:, :, :].rearrange("p k t -> p (k t)"), p_ot[:, :]).then_inc(xnT_done, 1)
                        if c == 1 and (B - 2).ok:
                            b = B - 2
                            normalise(b, 1)
                            dve.wait_ge(ot_done, 2 * b.n + 2)
                            dve.wait_ge(xres_in[b.par], 16 * (b.half + 1))
                            wait(dve, x2_out[b.par], 16 * b.half)
                            wait(dve, xn_done, b.n - 1)
                            nc.vector.scalar_tensor_tensor(x2[b.par][:, :], o_sb[:, :], tanh_x[:, 0:1], xres[b.par][:, :],
                                                           ALU.mult, ALU.add).then_inc(x2_done, 1)
                            dve.wait_ge(x2_done, b.n + 1)
                            stats(b, x2[b.par][:, :], st2, mv2, stat2)
                        if c == 2 and (B - 3).ok:
                            b = B - 3
                            dve.wait_ge(lg_mm, b.n + 1)
                            nc.vector.tensor_copy(lg[:, :], p_ms[:, 0:NE + 1]).then_inc(lg_done, 1)
                            dve.wait_ge(lg_done, b.n + 1)
                            alone(dve, spare_d)
                            chain.inc(nc.vector.max(v8[:, :], lg[:, 0:NE]))
                            chain.wait(dve)
                            alone(dve, spare_d)
                            chain.inc(nc.vector.max_index(i8[:, :], v8[:, :], lg[:, 0:NE]))
                            nc.vector.tensor_copy(top_val[:, bass.ts(b.n, TOPK)], v8[:, 0:TOPK])
                            nc.vector.tensor_copy(gate_z[:, bass.ts(b.n, 1)], lg[:, NE:NE + 1])
                            chain.wait(dve)
                            nc.vector.tensor_copy(top_idx[:, bass.ts(b.n, TOPK)], i8[:, 0:TOPK])
                            chain.inc(nc.vector.tensor_copy(idxf[:, :], i8[:, 0:TOPK]))
                            chain.wait(dve)
                            chain.inc(nc.vector.tensor_tensor(eqs[:, :, :], iota_e[:, :].unsqueeze(1).to_broadcast([128, TOPK, NE]),
                                                              idxf[:, :].unsqueeze(2).to_broadcast([128, TOPK, NE]), ALU.is_equal))
                            chain.wait(dve)
                            chain.inc(nc.vector.tensor_reduce(chosen[:, bass.ts(b.n, 1), :].rearrange("p a e -> p (a e)"),
                                                              eqs[:, :, :].rearrange("p k e -> p e k"), AX.X, ALU.add))
                            chain.wait(dve)
                        if c == 3 and (B - 1).ok:
                            normalise(B - 1, 0)
                chain.per_turn = 2 * (1 + 2 + 1 + 5)
                iterations(dve, body, chain)

            @block.tensor
            def _(pe):
                pe.wait_ge(consts, 1)
                pe.wait_ge(wr_in, 32)
                pe.wait_ge(pads, 8)
                mm, tr = nc.tensor.matmul, nc.tensor.transpose

                def k_cols(b):
                    pe.wait_ge(ks_done, b.n + 1)
                    wait(pe, mt_done, 4 * b.n - 1)
                    wait(pe, lg_done, b.n - 3)
                    for c in range(NC):
                        last = tr(p_ms[:, 128 * c:128 * c + 128], ks[:, 2 * c:2 * c + 2, :].rearrange("p g r -> p (g r)"), ident[:, :])
                    last.then_inc(k_mm, 1)

                def q_cols(b, c):
                    pe.wait_ge(qs_done, b.n + 1)
                    wait(pe, tq_done, 4 * b.n + c)
                    for i in range(G):
                        last = tr(p_tq[:, 128 * i:128 * i + 128], qs[b.par][:, c, i, :, :].rearrange("p g r -> p (g r)"), ident[:, :])
                    last.then_inc(tq_mm, 1)

                def pv(b, s):
                    pe.wait_ge(exp_done, 4 * b.n + 2 * s + 2)
                    if s == 0:
                        pe.wait_ge(v_in[b.par], 16 * (b.half + 1))
                    wait(pe, pv_done, 2 * b.n + s)
                    for q in range(4):
                        g = 4 * s + q
                        last = mm(p_pv[32 * q:32 * q + 32, :], vals[b.par][:, g, :],
                                  probs[2 * s + q // 2][:, 512 * (q % 2):512 * (q % 2) + 512], start=True, stop=True)
                    last.then_inc(pv_mm, 1)

                def o_cols(b, s):
                    pe.wait_ge(pv_done, 2 * b.n + s + 1)
                    wait(pe, ot_done, 2 * b.n + s)
                    for i in range(G):
                        last = tr(p_ot[:, 128 * i:128 * i + 128], ot_sb[s][:, 128 * i:128 * i + 128], ident[:, :])
                    last.then_inc(ot_mm, 1)

                def body(B):
                    if isinstance(B.n, int) and B.n == 0:
                        k_cols(B)
                        q_cols(B, 0)
                    for c in range(NC):
                        b = B - 1
                        if b.ok:
                            pe.wait_ge(mrow_in[c % 2], 32 * (2 * b.n + c // 2 + 1))
                            wait(pe, exp_done, 4 * b.n + c)
                            for g2 in range(2):
                                last = mm(p_exp[:, g2, :], kt[b.par][:, c, 128 * g2:128 * g2 + 128], qt[b.par][:, c, :],
                                          start=True, stop=True)
                            last.then_inc(p2_mm, 1)
                        if c == 0 and (B - 3).ok:
                            b = B - 3
                            pe.wait_ge(xn_done, b.n + 1)
                            pe.wait_ge(ot_done, 2 * b.n + (3 if (b + 1).ok else 2))
                            for k in range(KC):
                                last = tr(p_ot[:, 128 * k:128 * k + 128], xn[b.par][:, 128 * k:128 * k + 128], ident[:, :])
                            last.then_inc(xnT_mm, 1)
                        if c == 0 and (B - 2).ok:
                            pv(B - 2, 1)
                        if c == 2 and (B - 1).ok:
                            pv(B - 1, 0)
                        if c == 1 and (B - 2).ok:
                            if (B - 3).ok:
                                pe.wait_ge(xnT_done, (B - 3).n + 1)
                            o_cols(B - 2, 1)
                        if c == 3 and (B - 1).ok:
                            o_cols(B - 1, 0)
                        b, cc = (B - 1, 3) if c == 0 else (B, c - 1)
                        if b.ok:
                            pe.wait_ge(max_done, 4 * b.n + cc + 1)
                            wait(pe, mt_done, 4 * b.n + cc)
                            if cc == 3 and (b + 1).ok:
                                pe.wait_ge(kt_done, b.n + 2)
                            if cc == 2:
                                wait(pe, lg_done, b.n - 2)
                            last = tr(p_ms[0:8, 0:128], negmax[cc % 2][:, :], ident[:, :])
                            last.then_inc(mt_mm, 1)
                        if c == 2 and (B - 3).ok:
                            b = B - 3
                            pe.wait_ge(xnT_done, b.n + 1)
                            pe.wait_ge(mt_done, 4 * B.n + 2 if B.ok else 4 * NB)
                            wait(pe, lg_done, b.n)
                            for k in range(KC):
                                last = mm(p_ms[:, 0:NE + 1], xnT[b.par][:, k, :], wr[:, k, :], start=(k == 0), stop=(k == KC - 1))
                            last.then_inc(lg_mm, 1)
                        if c == 3 and (B + 1).ok:
                            k_cols(B + 1)
                        if c < 3 and B.ok:
                            q_cols(B, c + 1)
                        if c == 3 and (B + 1).ok:
                            q_cols(B + 1, 0)
                        if B.ok:
                            pe.wait_ge(tq_done, 4 * B.n + c + 1)
                            pe.wait_ge(kt_done, B.n + 1)
                            wait(pe, max_done, 4 * B.n + c)
                            for i in range(G):
                                last = mm(p_max[:, i // 2, 256 * (i % 2):256 * (i % 2) + 256], qt[B.par][:, c, 128 * i:128 * i + 128],
                                          kt[B.par][:, c, :], start=True, stop=True)
                            last.then_inc(p1_mm, 1)
                iterations(pe, body)

        with ExitStack() as scope:
            sb, ps, sem = maker(scope)
            WORK = 2048
            key_of = sb("key_of", [128, WORK])
            keys = sb("keys", [128, WORK])
            first = sb("first", [128, CAP])
            merge = sb("merge", [NE, 4 * CAP])
            firsts = sb("firsts", [NE, CAP])
            toks = sb("toks", [NE, CAP])
            halves = sb("halves", [CAP, 2, NPAIR])
            dv = sb("dv", [128, NB, TOPK])
            wsum, wrec = sb("wsum", [128, NB]), sb("wrec", [128, NB])
            route = sb("route", [128, NB, 2 * TOPK])
            zc, ez, ez1, sg = sb("zc", [128, NB]), sb("ez", [128, NB]), sb("ez1", [128, NB]), sb("sg", [128, NB])
            p_key = ps("p_key", [128, 4, 512])
            p_tok = ps("p_tok", [128, 512])
            iota_done, key_mm, tok_mm, toks_done = sem("iota_done"), sem("key_mm"), sem("tok_mm"), sem("toks_done")
            dv_done, ew_done, route_done, route_out, seq = sem("dv_done"), sem("ew_done"), sem("route_done"), sem("route_out"), sem("r_seq")
            block = scope.enter_context(nc.Block())

            @block.gpsimd
            def _(pool):
                for q in range(4):
                    nc.gpsimd.iota(key_of[32 * q:32 * q + 32, :], pattern=[[-4 * S, NB // 4], [-1, S]], base=TOK - S * q,
                                   channel_multiplier=0, allow_small_or_imprecise_dtypes=True).then_inc(iota_done, 1)

            @block.tensor
            def _(pe):
                for b in range(NB // 4):
                    last = nc.tensor.transpose(p_key[:, b // 4, 128 * (b % 4):128 * (b % 4) + 128],
                                               chosen[:, 4 * b:4 * b + 4, :].rearrange("p q e -> p (q e)"), ident[:, :])
                last.then_inc(key_mm, 1)
                pe.wait_ge(toks_done, 1)
                nc.tensor.transpose(p_tok[0:CAP, 0:NE], toks[:, :], ident[0:NE, 0:NE]).then_inc(tok_mm, 1)

            @block.scalar
            def _(act):
                act.wait_ge(dv_done, 1)
                nc.scalar.activation(route[:, :, TOPK:2 * TOPK], dv[:, :, :], ACT.Exp).then_inc(ew_done, 1)
                nc.scalar.activation(ez[:, :], zc[:, :], ACT.Exp, scale=-1.0).then_inc(ew_done, 1)

            @block.vector
            def _(dve):
                chain = Count(seq)

                def link(ins):
                    chain.inc(ins)
                    chain.wait(dve)

                nc.vector.tensor_scalar(zc[:, :], gate_z[:, :], -87.0, None, ALU.max)
                tv = top_val[:, :].rearrange("p (b k) -> p b k", k=TOPK)
                nc.vector.tensor_tensor(dv[:, :, :], tv, tv[:, :, 0:1].to_broadcast([128, NB, TOPK]), ALU.subtract).then_inc(dv_done, 1)
                nc.vector.tensor_copy(route[:, :, 0:TOPK], top_idx[:, :].rearrange("p (b k) -> p b k", k=TOPK))
                dve.wait_ge(ew_done, 2)
                link(nc.vector.tensor_reduce(wsum[:, :], route[:, :, TOPK:2 * TOPK], AX.X, ALU.add))
                link(nc.vector.reciprocal(wrec[:, :], wsum[:, :]))
                nc.vector.tensor_tensor(route[:, :, TOPK:2 * TOPK], route[:, :, TOPK:2 * TOPK],
                                        wrec[:, :].unsqueeze(2).to_broadcast([128, NB, TOPK]), ALU.mult).then_inc(route_done, 1)
                link(nc.vector.tensor_scalar(ez1[:, :], ez[:, :], 1.0, None, ALU.add))
                link(nc.vector.reciprocal(sg[:, :], ez1[:, :]))
                nc.vector.tensor_scalar(gate_s[:, :], sg[:, :], tanh_f[:, 0:1], None, ALU.mult)
                dve.wait_ge(iota_done, 4)
                dve.wait_ge(key_mm, 1)
                link(nc.vector.tensor_tensor(keys[:, :], p_key[:, :, :].rearrange("p a b -> p (a b)"), key_of[:, :], ALU.mult))
                for r in range(CAP // 8):
                    link(nc.vector.max(first[:, 8 * r:8 * r + 8], keys[:, :]))
                    if r < CAP // 8 - 1:
                        link(nc.vector.match_replace(keys[:, :], first[:, 8 * r:8 * r + 8], keys[:, :], 0.0))
                for q in range(4):
                    chain.inc(nc.vector.tensor_copy(merge[:, CAP * q:CAP * q + CAP], first[32 * q:32 * q + 32, :]))
                chain.wait(dve)
                for r in range(CAP // 8):
                    link(nc.vector.max(firsts[:, 8 * r:8 * r + 8], merge[:, :]))
                    if r < CAP // 8 - 1:
                        link(nc.vector.match_replace(merge[:, :], firsts[:, 8 * r:8 * r + 8], merge[:, :], 0.0))
                nc.vector.tensor_scalar(toks[:, :], firsts[:, :], -1.0, float(TOK), ALU.mult, ALU.add).then_inc(toks_done, 1)
                dve.wait_ge(tok_mm, 1)
                pt = p_tok[0:CAP, 0:NE].rearrange("c (i h) -> c h i", h=2)
                link(nc.vector.tensor_copy(halves[:, :, :], pt))
                nc.vector.tensor_copy(half_tok[:, :, :], halves[:, :, :])
                nc.vector.tensor_scalar(half_idx[:, :, :], halves[:, :, :], float(TOK - 1), None, ALU.min)
                nc.vector.tensor_scalar(half_used[:, :, :], halves[:, :, :], float(TOK), None, ALU.is_lt)
                for h in range(2):
                    nc.vector.tensor_scalar(slot_idx[CAP * h:CAP * h + CAP, :], halves[:, h, :], float(TOK - 1), None, ALU.min)

            @block.sync
            def _(sp):
                sp.wait_ge(route_done, 1)
                sp.dma_start(rw_dram.rearrange("(b t) c -> t b c", t=S), route[:, :, :]).then_inc(route_out, 16)
                sp.wait_ge(route_out, 16)

        routing.close()

        with ExitStack() as scope:
            sb, ps, sem = maker(scope)
            wgu_h = sb("wgu_h", [128, 2, KC, FS], F32R)
            wgu_l = sb("wgu_l", [128, 2, KC, FS], F32R)
            wd_h = sb("wd_h", [128, FC, E], F32R)
            wd_l = sb("wd_l", [128, FC, E], F32R)
            xraw = sb("xraw", [128, KC, TILE])
            xh = sb("xh", [128, KC, TILE], F32R)
            xl = sb("xl", [128, KC, TILE], F32R)
            act_f = sb("act_f", [128, TILE])
            hh = [sb(f"hh{i}", [128, TILE], F32R) for i in range(2)]
            hl = [sb(f"hl{i}", [128, TILE], F32R) for i in range(2)]
            rows = sb("rows", [128, TB, E])
            ew = sb("ew", [128, 2 * 2 * KC * FE])
            egu = ew[:, :].rearrange("p (h w k f) -> p h w k f", h=2, w=2, k=KC)
            edn = ew[:, 0:2 * 3 * E].rearrange("p (h c n) -> p h c n", h=2, c=3)
            xe = sb("xe", [128, E])
            xeT = sb("xeT", [128, KC, 128])
            eh = sb("eh", [128, FE])
            ehT = sb("ehT", [128, 3, 128])
            eo = sb("eo", [CAP, E])
            y1 = xe[0:CAP, :]
            cur_idx = sb("cur_idx", [128, 1], U32)
            cur_tok = [sb(f"cur_tok{h}", [CAP, 1], U32) for h in range(2)]
            cur_w = sb("cur_w", [CAP, 2])
            cur_g = sb("cur_g", [128, TB])
            rwg = sb("rwg", [CAP, NE, 2 * TOPK])
            gidx = [sb(f"gidx{i}", [CAP, 1], U32) for i in range(4)]
            e_of = sb("e_of", [CAP, NE])
            weq = ehT[0:CAP, 0, :].rearrange("p (e k) -> p e k", k=TOPK)
            w_slot = sb("w_slot", [CAP, 2, NPAIR])

            acc = ps("acc", [128, TB, 512])
            p_g, p_u = ps("p_g", [128, 512]), ps("p_u", [128, 512])
            p_x, p_y = ps("p_x", [128, 512]), ps("p_y", [128, 512])

            wraw_in = [sem(f"wraw_in{i}") for i in range(4)]
            whi_done, wlo_done = sem("whi_done"), sem("wlo_done")
            xraw_in, xhi_done, xlo_done = sem("xraw_in"), sem("xhi_done"), sem("xlo_done")
            g_mm, u_mm, dn_mm = sem("g_mm"), sem("u_mm"), sem("dn_mm")
            silu_done, h_done, hh_done, hl_done = sem("silu_done"), sem("h_done"), sem("hh_done"), sem("hl_done")
            rows_in, rows_out, add_done, gcur = sem("rows_in"), sem("rows_out"), sem("add_done"), sem("gcur")
            egu_in, edn_in = sem("egu_in"), sem("edn_in")
            xe_in, xeT_mm, xeT_done, eg_mm, eu_mm = sem("xe_in"), sem("xeT_mm"), sem("xeT_done"), sem("eg_mm"), sem("eu_mm")
            esilu_done, eh_done, ehT_mm, ehT_done, ed_mm = sem("esilu_done"), sem("eh_done"), sem("ehT_mm"), sem("ehT_done"), sem("ed_mm")
            eo_in, eo_out, eo_done, y_done = sem("eo_in"), sem("eo_out"), sem("eo_done"), sem("y_done")
            spare_p2, spare_s2 = sem("spare_p2"), sem("spare_s2")
            cur_set, wcur_set, eo_zero = sem("cur_set"), sem("wcur_set"), sem("eo_zero")
            rw_in = [sem(f"rw_in{i}") for i in range(4)]
            rw_set, eof_set, wchain = sem("rw_set"), sem("eof_set"), sem("wchain")

            SLOT = FS
            pieces = []
            for w, src in enumerate((Wsg, Wsu)):
                for k in range(KC):
                    pieces.append((src[128 * k:128 * k + 128, :], FS, wgu_h[:, w, k, :], wgu_l[:, w, k, :]))
            for f in range(0, FC, 2):
                n = min(2, FC - f)
                pieces.append((Wsd[128 * f:128 * (f + n), :].rearrange("(c p) n -> p c n", p=128), n * E,
                               wd_h[:, f:f + n, :].rearrange("p c n -> p (c n)"), wd_l[:, f:f + n, :].rearrange("p c n -> p (c n)")))
            NP = len(pieces)

            def staged(j):
                return ew[:, SLOT * (j % 4):SLOT * (j % 4) + pieces[j][1]]

            block = scope.enter_context(nc.Block())

            @block.sync
            def _(sp):
                def load_x(i):
                    sp.dma_start(xraw[:, :, :], xT_dram[:, :, bass.ts(i, TILE)].rearrange("k p t -> p k t")).then_inc(xraw_in, 16)

                def load_gate_up(i):
                    for h in range(2):
                        for w, src in enumerate((Wg, Wu)):
                            sp.dma_start(egu[:, h, w, :, :], src[2 * i + h].rearrange("(k p) f -> p k f", p=128)).then_inc(egu_in, 16)

                for j in range(NP):
                    wait(sp, wlo_done, j - 3)
                    n = pieces[j][1]
                    dst = staged(j) if n == FS else staged(j).rearrange("p (c n) -> p c n", n=E)
                    sp.dma_start(dst, pieces[j][0]).then_inc(wraw_in[j % 4], 16)
                    if j == 3:
                        load_x(0)
                sp.wait_ge(wlo_done, NP)
                load_gate_up(0)

                def body(i, last):
                    if not last:
                        sp.wait_ge(xlo_done, KC * i + KC)
                        load_x(i + 1)
                    sp.wait_ge(eu_mm, i + 1)
                    for h in range(2):
                        sp.dma_start(edn[:, h, 0:2, :], Wd[2 * i + h][0:256, :].rearrange("(c p) n -> p c n", p=128)).then_inc(edn_in, 16)
                        sp.dma_start(edn[0:FE - 256, h, 2, :], Wd[2 * i + h][256:FE, :]).then_inc(edn_in, 16)
                    sp.wait_ge(ed_mm, i + 1)
                    if not last:
                        load_gate_up(i + 1)
                    sp.wait_ge(eo_out, 32 * (i + 1))
                    sp.dma_start(rows[:, :, :], out_rows[bass.ts(i, TILE), :].rearrange("(j p) n -> p j n", p=128)).then_inc(rows_in, 16)
                    sp.wait_ge(add_done, TB * i + TB)
                    sp.dma_start(out_rows[bass.ts(i, TILE), :].rearrange("(j p) n -> p j n", p=128), rows[:, :, :]).then_inc(rows_out, 16)
                    sp.wait_ge(rows_out, 16 * (i + 1))
                    alone(sp, spare_s2)
                with sp.Fori(0, NT - 1) as i:
                    body(i, False)
                body(NT - 1, True)

            @block.gpsimd
            def _(pool):
                nc.gpsimd.memset(eo[:, :], 0.0).then_inc(eo_zero, 1)
                nc.gpsimd.iota(e_of[:, :], pattern=[[1, NE]], base=0, channel_multiplier=0,
                               allow_small_or_imprecise_dtypes=True).then_inc(eof_set, 1)
                for e in range(NE):
                    if e >= 4:
                        pool.wait_ge(rw_in[e % 4], 16 * (e // 4))
                    nc.gpsimd.tensor_copy(gidx[e % 4][:, :], half_idx[:, e % 2, e // 2:e // 2 + 1]).then_inc(rw_set, 1)
                    pool.wait_ge(rw_set, e + 1)
                    nc.gpsimd.indirect_dma_start(out=rwg[:, e, :], out_offset=None, in_=rw_dram,
                                                 in_offset=bass.IndirectOffsetOnAxis(ap=gidx[e % 4][:, 0:1], axis=0)).then_inc(rw_in[e % 4], 16)
                pool.wait_ge(eo_zero, 1)
                with pool.Fori(0, NT) as i:
                    pool.wait_ge(xeT_mm, i)
                    pool.wait_ge(eo_done, 2 * i)
                    alone(pool, spare_p2)
                    nc.gpsimd.tensor_copy(cur_idx[:, :], slot_idx[:, bass.ts(i, 1)])
                    for h in range(2):
                        last = nc.gpsimd.tensor_copy(cur_tok[h][:, :], half_tok[:, h, bass.ts(i, 1)])
                    last.then_inc(cur_set, 1)
                    pool.wait_ge(cur_set, i + 1)
                    alone(pool, spare_p2)
                    nc.gpsimd.indirect_dma_start(out=xe[:, :], out_offset=None, in_=xn_dram,
                                                 in_offset=bass.IndirectOffsetOnAxis(ap=cur_idx[:, 0:1], axis=0)).then_inc(xe_in, 16)
                    pool.wait_ge(rows_out, 16 * i)
                    alone(pool, spare_p2)
                    for h in range(2):
                        nc.gpsimd.indirect_dma_start(out=eo[:, :], out_offset=None, in_=out_rows,
                                                     in_offset=bass.IndirectOffsetOnAxis(ap=cur_tok[h][:, 0:1], axis=0),
                                                     bounds_check=TOK - 1, oob_is_err=False).then_inc(eo_in, 16)
                        pool.wait_ge(eo_done, 2 * i + h + 1)
                        alone(pool, spare_p2)
                        nc.gpsimd.indirect_dma_start(out=out_rows, out_offset=bass.IndirectOffsetOnAxis(ap=cur_tok[h][:, 0:1], axis=0),
                                                     in_=eo[:, :], in_offset=None,
                                                     bounds_check=TOK - 1, oob_is_err=False).then_inc(eo_out, 16)
                        pool.wait_ge(eo_out, 32 * i + 16 * h + 16)
                        alone(pool, spare_p2)

            @block.scalar
            def _(act):
                for j in range(NP):
                    act.wait_ge(wraw_in[j % 4], 16 * (j // 4 + 1))
                    nc.scalar.activation(pieces[j][2], staged(j), ACT.Copy).then_inc(whi_done, 1)

                def split_x(i):
                    act.wait_ge(xraw_in, 16 * (i + 1))
                    wait(act, u_mm, FC * i)
                    for k in range(KC):
                        nc.scalar.activation(xh[:, k, :], xraw[:, k, :], ACT.Copy).then_inc(xhi_done, 1)
                split_x(0)

                def body(i, last):
                    for f in range(FC):
                        act.wait_ge(g_mm, FC * i + f + 1)
                        wait(act, hl_done, FC * i + f)
                        nc.scalar.activation(act_f[:, :], p_g[:, :], ACT.Silu).then_inc(silu_done, 1)
                        if f == 0:
                            act.wait_ge(xeT_mm, i + 1)
                            nc.scalar.activation(xeT[:, :, :].rearrange("p k t -> p (k t)"), p_x[:, :], ACT.Copy).then_inc(xeT_done, 1)
                        if f == 1:
                            act.wait_ge(eg_mm, i + 1)
                            nc.scalar.activation(eh[:, :], p_y[:, 0:FE], ACT.Silu).then_inc(esilu_done, 1)
                        if f == 3:
                            act.wait_ge(ehT_mm, i + 1)
                            nc.scalar.activation(ehT[:, 0:2, :], p_y[:, 0:256].rearrange("p (c t) -> p c t", c=2), ACT.Copy)
                            nc.scalar.activation(ehT[0:FE - 256, 2, :], p_y[0:FE - 256, 256:384], ACT.Copy).then_inc(ehT_done, 1)
                    if not last:
                        split_x(i + 1)
                with act.Fori(0, NT - 1) as i:
                    body(i, False)
                body(NT - 1, True)

            @block.vector
            def _(dve):
                for j in range(NP):
                    dve.wait_ge(whi_done, j + 1)
                    nc.vector.tensor_tensor(pieces[j][3], staged(j), pieces[j][2].bitcast(F32), ALU.subtract).then_inc(wlo_done, 1)

                def split_x(i):
                    for k in range(KC):
                        dve.wait_ge(xhi_done, KC * i + k + 1)
                        nc.vector.tensor_tensor(xl[:, k, :], xraw[:, k, :], xh[:, k, :].bitcast(F32), ALU.subtract).then_inc(xlo_done, 1)
                split_x(0)
                for r in range(4):
                    dve.wait_ge(rw_in[r], 16 * (NE // 4))
                dve.wait_ge(eof_set, 1)
                chain = Count(wchain)

                def link(ins):
                    chain.inc(ins)
                    chain.wait(dve)
                link(nc.vector.tensor_tensor(weq[:, :, :], rwg[:, :, 0:TOPK], e_of[:, :].unsqueeze(2).to_broadcast([CAP, NE, TOPK]), ALU.is_equal))
                link(nc.vector.tensor_tensor(weq[:, :, :], weq[:, :, :], rwg[:, :, TOPK:2 * TOPK], ALU.mult))
                link(nc.vector.tensor_reduce(w_slot[:, :, :].rearrange("p h i -> p i h"), weq[:, :, :].rearrange("p (i h) k -> p i h k", h=2), AX.X, ALU.add))
                link(nc.vector.tensor_tensor(w_slot[:, :, :], w_slot[:, :, :], half_used[:, :, :], ALU.mult))
                link(nc.vector.tensor_scalar(w_slot[:, :, :], w_slot[:, :, :], tanh_f[0:CAP, 0:1], None, ALU.mult))

                def body(i, last):
                    for f in range(FC):
                        dve.wait_ge(silu_done, FC * i + f + 1)
                        dve.wait_ge(u_mm, FC * i + f + 1)
                        nc.vector.tensor_tensor(act_f[:, :], p_u[:, :], act_f[:, :], ALU.mult).then_inc(h_done, 1)
                        dve.wait_ge(h_done, FC * i + f + 1)
                        wait(dve, dn_mm, FC * i + max(f - 1, 0))
                        nc.vector.tensor_copy(hr(hh, f)[:, :], act_f[:, :]).then_inc(hh_done, 1)
                        dve.wait_ge(hh_done, FC * i + f + 1)
                        nc.vector.tensor_tensor(hr(hl, f)[:, :], act_f[:, :], hr(hh, f)[:, :].bitcast(F32), ALU.subtract).then_inc(hl_done, 1)
                        if f == 1:
                            dve.wait_ge(esilu_done, i + 1)
                            dve.wait_ge(eu_mm, i + 1)
                            nc.vector.tensor_tensor(eh[:, :], p_x[:, 0:FE], eh[:, :], ALU.mult).then_inc(eh_done, 1)
                        if f == 4:
                            nc.vector.tensor_copy(cur_w[:, :], w_slot[:, :, bass.ts(i, 1)].rearrange("p h a -> p (h a)"))
                            nc.vector.tensor_copy(cur_g[:, :], gate_s[:, bass.ts(i, TB)]).then_inc(wcur_set, 1)
                        if f == 5:
                            dve.wait_ge(wcur_set, i + 1)
                            dve.wait_ge(ed_mm, i + 1)
                            dve.wait_ge(eo_in, 32 * i + 16)
                            nc.vector.scalar_tensor_tensor(eo[:, :], p_x[0:CAP, :], cur_w[:, 0:1], eo[:, :], ALU.mult, ALU.add).then_inc(eo_done, 1)
                            nc.vector.tensor_copy(y1, p_x[CAP:2 * CAP, :]).then_inc(y_done, 1)
                        if f == 7:
                            dve.wait_ge(y_done, i + 1)
                            dve.wait_ge(eo_in, 32 * i + 32)
                            nc.vector.scalar_tensor_tensor(eo[:, :], y1, cur_w[:, 1:2], eo[:, :], ALU.mult, ALU.add).then_inc(eo_done, 1)
                    if not last:
                        split_x(i + 1)
                    dve.wait_ge(rows_in, 16 * (i + 1))
                    dve.wait_ge(dn_mm, FC * i + FC)
                    for j in range(TB):
                        nc.vector.scalar_tensor_tensor(rows[:, j, :], acc[:, j, :], cur_g[:, j:j + 1], rows[:, j, :],
                                                       ALU.mult, ALU.add).then_inc(add_done, 1)
                with dve.Fori(0, NT - 1) as i:
                    body(i, False)
                body(NT - 1, True)

            @block.tensor
            def _(pe):
                mm, tr = nc.tensor.matmul, nc.tensor.transpose

                def down(i, f):
                    pe.wait_ge(hl_done, FC * i + f + 1)
                    if f == 0:
                        pe.wait_ge(add_done, TB * i)
                    for j in range(TB):
                        t = slice(128 * j, 128 * j + 128)
                        a, b = hr(hh, f), hr(hl, f)
                        mm(acc[:, j, :], a[:, t], wd_h[:, f, :], start=(f == 0), stop=False)
                        mm(acc[:, j, :], a[:, t], wd_l[:, f, :], start=False, stop=False)
                        last = mm(acc[:, j, :], b[:, t], wd_h[:, f, :], start=False, stop=(f == FC - 1))
                    last.then_inc(dn_mm, 1)

                pe.wait_ge(wlo_done, NP)

                def body(i):
                    for f in range(FC):
                        cols = slice(128 * f, 128 * f + 128)
                        for w, bank, done, free in ((0, p_g, g_mm, silu_done), (1, p_u, u_mm, h_done)):
                            wait(pe, free, FC * i + f)
                            for k in range(KC):
                                if f == 0 and w == 0:
                                    pe.wait_ge(xlo_done, KC * i + k + 1)
                                mm(bank[:, :], wgu_h[:, w, k, cols], xh[:, k, :], start=(k == 0), stop=False)
                                mm(bank[:, :], wgu_h[:, w, k, cols], xl[:, k, :], start=False, stop=False)
                                last = mm(bank[:, :], wgu_l[:, w, k, cols], xh[:, k, :], start=False, stop=(k == KC - 1))
                            last.then_inc(done, 1)
                        if f == 0:
                            pe.wait_ge(xe_in, 16 * (i + 1))
                            wait(pe, y_done, i)
                            for k in range(KC):
                                last = tr(p_x[:, 128 * k:128 * k + 128], xe[:, 128 * k:128 * k + 128], ident[:, :])
                            last.then_inc(xeT_mm, 1)
                        if f == 1:
                            pe.wait_ge(xeT_done, i + 1)
                            pe.wait_ge(egu_in, 64 * (i + 1))
                            for w, bank, done in ((0, p_y, eg_mm), (1, p_x, eu_mm)):
                                for k in range(KC):
                                    for h in range(2):
                                        last = mm(bank[CAP * h:CAP * h + CAP, 0:FE], xeT[:, k, CAP * h:CAP * h + CAP], egu[:, h, w, k, :],
                                                  start=(k == 0), stop=(k == KC - 1))
                                last.then_inc(done, 1)
                        if f == 3:
                            pe.wait_ge(eh_done, i + 1)
                            for c, (a, n) in enumerate(FEC):
                                last = tr(p_y[0:n, 128 * c:128 * c + 128], eh[:, a:a + n], ident[:, :])
                            last.then_inc(ehT_mm, 1)
                        if f == 5:
                            pe.wait_ge(ehT_done, i + 1)
                            pe.wait_ge(edn_in, 64 * (i + 1))
                            for c, (a, n) in enumerate(FEC):
                                for h in range(2):
                                    last = mm(p_x[CAP * h:CAP * h + CAP, :], ehT[0:n, c, CAP * h:CAP * h + CAP], edn[0:n, h, c, :],
                                              start=(c == 0), stop=(c == len(FEC) - 1))
                            last.then_inc(ed_mm, 1)
                        if f > 0:
                            down(i, f - 1)
                    down(i, FC - 1)
                with pe.Fori(0, NT) as i:
                    body(i)


def hr(pair, f):
    return pair[f % 2]


_INS = ['x', 'ctx_512', 'g_xattn', 'g_ffn', 'L0_ffn_Wr', 'L0_ffn_Wg', 'L0_ffn_Wu', 'L0_ffn_Wd', 'L0_ffn_Wsg', 'L0_ffn_Wsu',
        'L0_ffn_Wsd', 'L0_ffn_Wse']
_OUTS = [((NB, S, E), 'float32')]


def kernel(**inputs):
    import numpy as _np
    import concourse.bacc as _bacc
    from concourse import mybir as _mybir
    from concourse.bass_utils import run_bass_kernel_spmd as _run

    nc = _bacc.Bacc("TRN2", target_bir_lowering=False, num_devices=1)
    arrays, args = {}, []
    for name in _INS:
        a = _np.ascontiguousarray(inputs[name])
        arrays[f"in_{name}_dram"] = a
        args.append(nc.dram_tensor(f"in_{name}_dram", a.shape, _mybir.dt.from_np(a.dtype), kind="ExternalInput").ap())
    for i, (shape, dtype) in enumerate(_OUTS):
        dt = _mybir.dt.from_np(_np.dtype(dtype))
        args.append(nc.dram_tensor(f"out_{i}_dram", shape, dt, kind="ExternalOutput").ap())
    build(nc, *args)
    r = _run(nc, [arrays], core_ids=[0])
    got = tuple(r.results[0][f"out_{i}_dram"] for i in range(len(_OUTS)))
    return got[0]
```

```python
import concourse.bass as bass
from concourse import mybir
from contextlib import ExitStack

F32 = mybir.dt.float32
F32R = mybir.dt.float32r
U32 = mybir.dt.uint32
I32 = mybir.dt.int32
ALU = mybir.AluOpType
ACT = mybir.ActivationFunctionType
AX = mybir.AxisListType

NB, S, E = 64, 128, 512
NH, NKV, D = 32, 8, 16
G = NH // NKV
KC = E // 128
TOK = NB * S
NE, TOPK, CAP = 32, 4, 64
FE, FS = 352, 1408
FC = FS // 128
EPS = 1e-5
NC = 4
TILE = 512
NT = TOK // TILE
TB = TILE // S
NPAIR = NE // 2
FEC = [(0, 128), (128, 128), (256, FE - 256)]


def wait(eng, sem, value):
    if not isinstance(value, int) or value > 0:
        eng.wait_ge(sem, value)


def alone(eng, sem):
    eng.sem_inc(sem, 1)


class Count:

    def __init__(self, sem):
        self.sem, self.at, self.base, self.turn = sem, 0, 0, 0

    def inc(self, ins, n=1):
        self.at += n
        ins.then_inc(self.sem, n)

    def value(self):
        return self.base + self.at + self.turn

    def wait(self, eng):
        eng.wait_ge(self.sem, self.value())


class Batch:

    def __init__(self, pair, off):
        self.pair, self.off = pair, off

    def __add__(self, n):
        return Batch(self.pair, self.off + n)

    def __sub__(self, n):
        return Batch(self.pair, self.off - n)

    @property
    def n(self):
        return 2 * self.pair + self.off

    @property
    def half(self):
        return self.pair + self.off // 2

    @property
    def par(self):
        return self.off % 2

    @property
    def ok(self):
        return not isinstance(self.pair, int) or 0 <= self.n < NB


def build(nc, x, ctx_in, g_xattn, g_ffn, Wr, Wg, Wu, Wd, Wsg, Wsu, Wsd, Wse, out):
    x_t = x
    out_rows = out.rearrange("b s e -> (b s) e")
    xn_dram = nc.dram_tensor("xn_rows", (TOK, E), F32, kind="Internal").ap()
    xT_dram = nc.dram_tensor("xn_cols", (KC, 128, TOK), F32, kind="Internal").ap()
    rw_dram = nc.dram_tensor("route_rows", (TOK, 2 * TOPK), F32, kind="Internal").ap()

    stack = ExitStack()
    with stack:
        def maker(scope):
            def sb(name, shape, dt=F32):
                return scope.enter_context(nc.sbuf_tensor(name, shape, dt))

            def ps(name, shape, dt=F32):
                return scope.enter_context(nc.psum_tensor(name, shape, dt))

            def sem(name):
                return scope.enter_context(nc.semaphore(name))
            return sb, ps, sem

        sb, _, sem = maker(stack)
        ident = sb("ident", [128, 128])
        tanh_x = sb("tanh_x", [128, 1])
        tanh_f = sb("tanh_f", [128, 1])
        slot_idx = sb("slot_idx", [128, NPAIR], U32)
        half_idx = sb("half_idx", [CAP, 2, NPAIR], U32)
        half_tok = sb("half_tok", [CAP, 2, NPAIR], U32)
        half_used = sb("half_used", [CAP, 2, NPAIR])
        gate_s = sb("gate_s", [128, NB])
        routing = stack.enter_context(ExitStack())
        sb, _, _ = maker(routing)
        top_val = sb("top_val", [128, NB * TOPK])
        top_idx = sb("top_idx", [128, NB * TOPK])
        gate_z = sb("gate_z", [128, NB])

        with ExitStack() as scope:
            sb, ps, sem = maker(scope)
            xs = [sb(f"xs{i}", [128, E]) for i in range(2)]
            xres = [sb(f"xres{i}", [128, E]) for i in range(2)]
            kv = [sb(f"kv{i}", [128, NKV * D]) for i in range(2)]
            vals = [sb(f"vals{i}", [128, NKV, 32]) for i in range(2)]
            ks = sb("ks", [128, NKV, 64])
            qraw = [sb(f"qraw{i}", [128, E]) for i in range(2)]
            qs = [sb(f"qs{i}", [128, NC, G, 2, 64]) for i in range(2)]
            qt = [sb(f"qt{i}", [128, NC, G * 128], F32R) for i in range(2)]
            kt = [sb(f"kt{i}", [128, NC, 2 * 128], F32R) for i in range(2)]
            probs = [sb(f"probs{i}", [128, 2 * 512]) for i in range(4)]
            ot_sb = [sb(f"ot_sb{i}", [128, 512]) for i in range(2)]
            o_sb = sb("o_sb", [128, E])
            rec = sb("rec", [128, 16])
            x2 = [sb(f"x2_{i}", [128, E]) for i in range(2)]
            xn = [sb(f"xn_{i}", [128, E]) for i in range(2)]
            xnT = [sb(f"xnT{i}", [128, KC, 128]) for i in range(2)]
            wr = sb("wr", [128, KC, NE + 1])
            negmax = [sb(f"negmax{i}", [128, 8]) for i in range(2)]
            mt = [sb(f"mt{i}", [8, 128], F32R) for i in range(2)]
            st1, st2 = sb("st1", [128, 6]), sb("st2", [128, 6])
            mv1 = [sb(f"mv1_{i}", [128, 2]) for i in range(2)]
            mv2 = [sb(f"mv2_{i}", [128, 2]) for i in range(2)]
            ve1, rs1 = sb("ve1", [128, 1]), sb("rs1", [128, 1])
            ve2, rs2 = sb("ve2", [128, 1]), sb("rs2", [128, 1])
            mhalf = sb("mhalf", [128, 1])
            lg = sb("lg", [128, NE + 1])
            v8 = sb("v8", [128, 8])
            i8 = sb("i8", [128, 8], U32)
            gx, gf = sb("gx", [128, 1]), sb("gf", [128, 1])

            p_max = ps("p_max", [128, 2, 512])
            p_exp = ps("p_exp", [128, 2, 512])
            p_tq = ps("p_tq", [128, 512])
            p_pv = ps("p_pv", [128, 512])
            p_ot = ps("p_ot", [128, 512])
            p_mt = ps("p_mt", [8, 128])

            x_in = [sem(f"x_in{i}") for i in range(2)]
            kv_in = [sem(f"kv_in{i}") for i in range(2)]
            xres_in = [sem(f"xres_in{i}") for i in range(2)]
            v_in = [sem(f"v_in{i}") for i in range(2)]
            mrow_in = [sem(f"mrow_in{i}") for i in range(2)]
            x2_out = [sem(f"x2_out{i}") for i in range(2)]
            xn_out = [sem(f"xn_out{i}") for i in range(2)]
            xnT_out = [sem(f"xnT_out{i}") for i in range(2)]
            wr_in, g_in = sem("wr_in"), sem("g_in")
            spare_d, spare_p, spare_s = sem("spare_d"), sem("spare_p"), sem("spare_s")
            consts, tanh_done = sem("consts"), sem("tanh_done")
            pads, id0 = sem("pads"), sem("id0")
            rs1_done, rs2_done, qraw_done = sem("rs1_done"), sem("rs2_done"), sem("qraw_done")
            top_done, kept = sem("top_done"), sem("kept")
            stat1, stat2 = sem("stat1"), sem("stat2")
            ks_done, qs_done, xn_done = sem("ks_done"), sem("qs_done"), sem("xn_done")
            pool_chain, dve_chain = sem("pool_chain"), sem("dve_chain")
            tq_mm, k_mm, p1_mm, p2_mm = sem("tq_mm"), sem("k_mm"), sem("p1_mm"), sem("p2_mm")
            pv_mm, ot_mm, mt_mm = sem("pv_mm"), sem("ot_mm"), sem("mt_mm")
            xnT_mm, lg_mm = sem("xnT_mm"), sem("lg_mm")
            max_done, exp_done, tq_done = sem("max_done"), sem("exp_done"), sem("tq_done")
            kt_done, pv_done, mt_done = sem("kt_done"), sem("pv_done"), sem("mt_done")
            ot_done, x2_done, xnT_done, lg_done = sem("ot_done"), sem("x2_done"), sem("xnT_done"), sem("lg_done")

            FIRST, LAST = 5, 61

            def iterations(eng, body, count=None):
                for b in range(FIRST):
                    body(Batch((b - 1) // 2, b - 2 * ((b - 1) // 2)))
                start = count.at if count else 0
                with eng.Fori((FIRST - 1) // 2, (LAST - 1) // 2) as pair:
                    if count:
                        count.turn = (pair - (FIRST - 1) // 2) * count.per_turn
                    body(Batch(pair, 1))
                    body(Batch(pair, 2))
                if count:
                    assert count.at - start == count.per_turn, count.at - start
                    count.turn = 0
                    count.at = start + count.per_turn * ((LAST - FIRST) // 2)
                for b in range(LAST, NB + 4):
                    body(Batch((b - 1) // 2, b - 2 * ((b - 1) // 2)))

            block = scope.enter_context(nc.Block())

            @block.sync
            def _(sp):
                sp.dma_start(wr[:, :, 0:NE], Wr.rearrange("(k p) e -> p k e", p=128)).then_inc(wr_in, 16)
                sp.dma_start(wr[:, :, NE:NE + 1], Wse.rearrange("(k p) e -> p k e", p=128),
                             allow_slow_non_contiguous=True).then_inc(wr_in, 16)
                sp.dma_start(gx[:, :], g_xattn.rearrange("(a n) -> a n", a=1).to_broadcast([128, 1])).then_inc(g_in, 16)
                sp.dma_start(gf[:, :], g_ffn.rearrange("(a n) -> a n", a=1).to_broadcast([128, 1])).then_inc(g_in, 16)

                def load_in(b):
                    wait(sp, qraw_done, b.n - 1)
                    sp.dma_start(xs[b.par][:, :], x_t[b.n]).then_inc(x_in[b.par], 16)
                    wait(sp, ks_done, b.n - 1)
                    sp.dma_start(kv[b.par][:, :], ctx_in[b.n]).then_inc(kv_in[b.par], 16)

                def body(B):
                    if isinstance(B.n, int) and B.n == 0:
                        load_in(B)
                        load_in(B + 1)
                        load_in(B + 2)
                    for c in range(NC):
                        m = (B - 1, 3) if c == 0 else (B, c - 1)
                        if m[0].ok:
                            b, cc = m
                            wait(sp, mt_done, 4 * b.n + cc + 1)
                            for g2 in range(2):
                                sp.dma_start(qt[b.par][64 * g2:64 * g2 + 1, cc, :].bitcast(F32),
                                             mt[cc % 2][4 * g2:4 * g2 + 4, :].bitcast(F32)).then_inc(mrow_in[cc % 2], 16)
                        if c == 0:
                            if (B - 1).ok:
                                wait(sp, x2_done, (B - 1).n - 1)
                                sp.dma_start(xres[(B - 1).par][:, :], x_t[(B - 1).n]).then_inc(xres_in[(B - 1).par], 16)
                            if (B - 3).ok:
                                b = B - 3
                                wait(sp, xn_done, b.n + 1)
                                sp.dma_start(xn_dram[bass.ts(b.n, 128), :], xn[b.par][:, :]).then_inc(xn_out[b.par], 16)
                        if c == 1:
                            if (B + 3).ok:
                                load_in(B + 3)
                            if B.ok:
                                wait(sp, pv_mm, 2 * (B.n - 1))
                                if isinstance(B.n, int) and B.n < 2:
                                    sp.wait_ge(pads, 4)
                                sp.dma_start(vals[B.par][:, :, 0:D], ctx_in[B.n].rearrange("t (g d) -> t g d", d=D)).then_inc(v_in[B.par], 16)
                            if (B - 3).ok:
                                b = B - 3
                                wait(sp, xnT_done, b.n + 1)
                                alone(sp, spare_s)
                                sp.dma_start(xT_dram[:, :, bass.ts(b.n, 128)].rearrange("k p t -> p k t"), xnT[b.par][:, :, :]).then_inc(xnT_out[b.par], 16)
                        if c == 2 and (B - 2).ok:
                            b = B - 2
                            wait(sp, x2_done, b.n + 1)
                            sp.dma_start(out_rows[bass.ts(b.n, 128), :], x2[b.par][:, :]).then_inc(x2_out[b.par], 16)
                iterations(sp, body)
                for s in (x2_out, xn_out, xnT_out):
                    for i in range(2):
                        sp.wait_ge(s[i], 16 * (NB // 2))

            @block.gpsimd
            def _(pool):
                nc.gpsimd.memset(ident[:, :], 0.0).then_inc(id0, 1)
                pool.wait_ge(id0, 1)
                nc.gpsimd.affine_select(out=ident[:, :], in_=ident[:, :], compare_op=ALU.not_equal, fill=1.0, base=0,
                                        pattern=[[-1, 128]], channel_multiplier=1).then_inc(consts, 1)
                nc.gpsimd.memset(mhalf[:, :], -0.5).then_inc(id0, 1)
                pool.wait_ge(id0, 2)
                pool.wait_ge(pads, 8)
                chain = Count(pool_chain)

                def inverse_root(b, stat, mv, ve, rs, used, done):
                    pool.wait_ge(stat, b.n + 1)
                    alone(pool, spare_p)
                    chain.inc(nc.gpsimd.tensor_scalar(ve[:, :], mv[b.par][:, 1:2], EPS, None, ALU.add))
                    chain.wait(pool)
                    wait(pool, used, b.n)
                    alone(pool, spare_p)
                    nc.gpsimd.tensor_tensor(rs[:, :], ve[:, :], mhalf[:, :], ALU.pow).then_inc(done, 1)

                def k_stacks(b):
                    pool.wait_ge(kv_in[b.par], 16 * (b.half + 1))
                    wait(pool, k_mm, b.n)
                    alone(pool, spare_p)
                    kin = kv[b.par][:, :].rearrange("p (g d) -> p g d", d=D)
                    nc.gpsimd.tensor_scalar(ks[:, :, 16:32].bitcast(F32R), kin, 1.0, 0.0, ALU.mult, ALU.add)
                    chain.inc(nc.gpsimd.tensor_scalar(ks[:, :, 48:64].bitcast(F32R), kin, 1.0, 0.0, ALU.mult, ALU.add))
                    chain.wait(pool)
                    nc.gpsimd.tensor_tensor(ks[:, :, 32:48], kin, ks[:, :, 16:32], ALU.subtract).then_inc(ks_done, 1)

                def q_stacks(b):
                    pool.wait_ge(qraw_done, b.n + 1)
                    wait(pool, tq_mm, 4 * (b.n - 1))
                    alone(pool, spare_p)

                    def stack(part, g2):
                        return qs[b.par][:, :, :, g2, 16 * part:16 * part + 16]

                    def heads(g2):
                        return qraw[b.par][:, :].rearrange("p (c g i d) -> p c g i d", g=2, i=G, d=D)[:, :, g2, :, :]

                    for part in (1, 2):
                        for g2 in range(2):
                            last = nc.gpsimd.tensor_scalar(stack(part, g2).bitcast(F32R), heads(g2), 1.0, 0.0, ALU.mult, ALU.add)
                    chain.inc(last)
                    chain.wait(pool)
                    for g2 in range(2):
                        last = nc.gpsimd.tensor_tensor(stack(3, g2), heads(g2), stack(1, g2), ALU.subtract)
                    last.then_inc(qs_done, 1)

                def body(B):
                    if isinstance(B.n, int) and B.n == 0:
                        inverse_root(B, stat1, mv1, ve1, rs1, qraw_done, rs1_done)
                        k_stacks(B)
                        q_stacks(B)
                        inverse_root(B + 1, stat1, mv1, ve1, rs1, qraw_done, rs1_done)
                    if (B + 1).ok:
                        k_stacks(B + 1)
                        q_stacks(B + 1)
                    if (B + 2).ok:
                        inverse_root(B + 2, stat1, mv1, ve1, rs1, qraw_done, rs1_done)
                    if (B - 2).ok:
                        inverse_root(B - 2, stat2, mv2, ve2, rs2, xn_done, rs2_done)
                    b = B - 4
                    if b.ok:
                        pool.wait_ge(top_done, b.n + 1)
                        alone(pool, spare_p)
                        nc.gpsimd.tensor_copy(top_val[:, bass.ts(b.n, TOPK)], v8[:, 0:TOPK])
                        nc.gpsimd.tensor_copy(gate_z[:, bass.ts(b.n, 1)], lg[:, NE:NE + 1])
                        nc.gpsimd.tensor_copy(top_idx[:, bass.ts(b.n, TOPK)], i8[:, 0:TOPK]).then_inc(kept, 1)

                chain.per_turn = 2 * (1 + 1 + 1 + 1)
                iterations(pool, body, chain)

            @block.scalar
            def _(act):
                act.wait_ge(g_in, 32)
                nc.scalar.activation(tanh_x[:, :], gx[:, :], ACT.Tanh).then_inc(tanh_done, 1)
                nc.scalar.activation(tanh_f[:, :], gf[:, :], ACT.Tanh).then_inc(tanh_done, 1)
                act.wait_ge(pads, 8)

                def k_evac(b):
                    act.wait_ge(k_mm, b.n + 1)
                    wait(act, p2_mm, 4 * (b.n - 1))
                    nc.scalar.activation(kt[b.par][0:64, :, 0:128], p_pv[0:64, :].rearrange("p (c t) -> p c t", c=NC), ACT.Copy)
                    nc.scalar.activation(kt[b.par][64:128, :, 128:256], p_pv[64:128, :].rearrange("p (c t) -> p c t", c=NC),
                                         ACT.Copy).then_inc(kt_done, 1)

                def q_evac(b, c):
                    act.wait_ge(tq_mm, 4 * b.n + c + 1)
                    wait(act, p2_mm, 4 * (b.n - 2) + c + 1)
                    nc.scalar.activation(qt[b.par][:, c, :], p_tq[:, :], ACT.Copy).then_inc(tq_done, 1)

                def pv_evac(b, s):
                    act.wait_ge(pv_mm, 2 * b.n + s + 1)
                    wait(act, ot_mm, 2 * (b.n - 1) + s + 1)
                    nc.scalar.activation(ot_sb[s][:, :], p_pv[:, :], ACT.Copy).then_inc(pv_done, 1)

                def body(B):
                    if isinstance(B.n, int) and B.n == 0:
                        k_evac(B)
                        q_evac(B, 0)
                    for c in range(NC):
                        b = B - 1
                        if b.ok:
                            act.wait_ge(p2_mm, 4 * b.n + c + 1)
                            wait(act, pv_mm, 2 * (b.n - 1) + c // 2 + 1)
                            nc.scalar.activation(probs[c][:, :], p_exp[:, :, :].rearrange("p a b -> p (a b)"), ACT.Exp,
                                                 scale=float(D) ** -0.5).then_inc(exp_done, 1)
                        if c == 1 and (B - 3).ok:
                            b = B - 3
                            act.wait_ge(xnT_mm, b.n + 1)
                            wait(act, xnT_out[b.par], 16 * b.half)
                            wait(act, lg_mm, b.n - 1)
                            nc.scalar.activation(xnT[b.par][:, :, :].rearrange("p k t -> p (k t)"), p_pv[:, :], ACT.Copy).then_inc(xnT_done, 1)
                        if c == 0 and (B - 2).ok:
                            pv_evac(B - 2, 1)
                        if c == 2 and (B - 1).ok:
                            pv_evac(B - 1, 0)
                        if c == 3 and (B + 1).ok:
                            k_evac(B + 1)
                        if c < 3 and B.ok:
                            q_evac(B, c + 1)
                        if c == 3 and (B + 1).ok:
                            q_evac(B + 1, 0)
                        b, cc = (B - 1, 3) if c == 0 else (B, c - 1)
                        if b.ok:
                            act.wait_ge(mt_mm, 4 * b.n + cc + 1)
                            wait(act, mrow_in[cc % 2], 32 * (2 * b.n + cc // 2))
                            nc.scalar.activation(mt[cc % 2][:, :], p_mt[:, :], ACT.Copy).then_inc(mt_done, 1)
                iterations(act, body)

            @block.vector
            def _(dve):
                for i in range(2):
                    nc.vector.memset(vals[i][:, :, 16:32], 0.0).then_inc(pads, 1)
                dve.wait_ge(pads, 2)
                for i in range(2):
                    nc.vector.memset(vals[i][:, :, 16:17], 1.0).then_inc(pads, 1)
                for i in range(2):
                    nc.vector.memset(qs[i][:, :, :, :, 0:16], 0.0).then_inc(pads, 1)
                nc.vector.memset(kt[0][:, :, :].bitcast(F32), 0.0)
                nc.vector.memset(kt[1][:, :, :].bitcast(F32), 0.0).then_inc(pads, 1)
                nc.vector.memset(ks[:, :, 0:16], 0.0).then_inc(dve_chain, 1)
                chain = Count(dve_chain)
                chain.at = 1
                chain.wait(dve)
                nc.vector.memset(ks[:, :, 0:1], 1.0).then_inc(pads, 1)
                dve.wait_ge(consts, 1)
                dve.wait_ge(tanh_done, 2)

                def stats(b, source, st, mv, done):
                    chain.inc(nc.vector.bn_stats(st[:, :], source))
                    chain.wait(dve)
                    alone(dve, spare_d)
                    nc.vector.bn_aggr(mv[b.par][:, :], st[:, :]).then_inc(done, 1)

                def stats_x(b):
                    dve.wait_ge(x_in[b.par], 16 * (b.half + 1))
                    stats(b, xs[b.par][:, :], st1, mv1, stat1)

                def layer_norm(b, source, mv, rs, ready, target, done):
                    dve.wait_ge(ready, b.n + 1)
                    nc.vector.tensor_scalar(target[b.par][:, :], source[b.par][:, :], mv[b.par][:, 0:1], rs[:, 0:1],
                                            ALU.subtract, ALU.mult).then_inc(done, 1)

                def norm_x(b):
                    wait(dve, qs_done, b.n - 1)
                    layer_norm(b, xs, mv1, rs1, rs1_done, qraw, qraw_done)

                def normalise(b, s):
                    dve.wait_ge(ot_mm, 2 * b.n + s + 1)
                    v = p_ot[:, :].rearrange("p (i q r) -> p i q r", i=G, q=4)
                    chain.inc(nc.vector.reciprocal(rec[:, :].rearrange("p (i q) -> p i q", i=G), v[:, :, :, D]))
                    chain.wait(dve)
                    if s == 0:
                        wait(dve, x2_done, b.n)
                    ov = o_sb[:, 256 * s:256 * s + 256].rearrange("p (q i d) -> p i q d", q=4, i=G)
                    rv = rec[:, :].rearrange("p (i q) -> p i q", i=G).unsqueeze(3).to_broadcast([128, G, 4, D])
                    nc.vector.tensor_tensor(ov, v[:, :, :, 0:D], rv, ALU.mult).then_inc(ot_done, 1)

                def body(B):
                    if isinstance(B.n, int) and B.n == 0:
                        stats_x(B)
                        norm_x(B)
                        stats_x(B + 1)
                    for c in range(NC):
                        if c == 2 and (B - 4).ok:
                            b = B - 4
                            dve.wait_ge(lg_mm, b.n + 1)
                            wait(dve, kept, b.n)
                            nc.vector.tensor_copy(lg[:, :], p_ot[:, 0:NE + 1]).then_inc(lg_done, 1)
                        if c == 1 and (B - 2).ok:
                            normalise(B - 2, 1)
                        if c == 3 and (B - 1).ok:
                            normalise(B - 1, 0)
                        if B.ok:
                            dve.wait_ge(p1_mm, 4 * B.n + c + 1)
                            wait(dve, mt_mm, 4 * B.n + c - 1)
                            nc.vector.tensor_reduce(negmax[c % 2][:, :].rearrange("p (g i) -> p i g", i=G),
                                                    p_max[:, :, :].rearrange("p a (h g t) -> p (a h) g t", g=2, t=128),
                                                    AX.X, ALU.max, negate=True).then_inc(max_done, 1)
                        if c == 0:
                            if (B + 1).ok:
                                norm_x(B + 1)
                            if (B + 2).ok:
                                stats_x(B + 2)
                        if c == 2 and (B - 2).ok:
                            b = B - 2
                            dve.wait_ge(ot_done, 2 * b.n + 2)
                            dve.wait_ge(xres_in[b.par], 16 * (b.half + 1))
                            wait(dve, x2_out[b.par], 16 * b.half)
                            nc.vector.scalar_tensor_tensor(x2[b.par][:, :], o_sb[:, :], tanh_x[:, 0:1], xres[b.par][:, :],
                                                           ALU.mult, ALU.add).then_inc(x2_done, 1)
                            dve.wait_ge(x2_done, b.n + 1)
                            stats(b, x2[b.par][:, :], st2, mv2, stat2)
                        if c == 3 and (B - 2).ok:
                            b = B - 2
                            wait(dve, xnT_mm, b.n - 1)
                            wait(dve, xn_out[b.par], 16 * b.half)
                            layer_norm(b, x2, mv2, rs2, rs2_done, xn, xn_done)
                        if c == 3 and (B - 4).ok:
                            b = B - 4
                            dve.wait_ge(lg_done, b.n + 1)
                            alone(dve, spare_d)
                            chain.inc(nc.vector.max(v8[:, :], lg[:, 0:NE]))
                            chain.wait(dve)
                            alone(dve, spare_d)
                            nc.vector.max_index(i8[:, :], v8[:, :], lg[:, 0:NE]).then_inc(top_done, 1)
                chain.per_turn = 2 * (1 + 1 + 1 + 1 + 1)
                iterations(dve, body, chain)

            @block.tensor
            def _(pe):
                pe.wait_ge(consts, 1)
                pe.wait_ge(wr_in, 32)
                pe.wait_ge(pads, 8)
                mm, tr = nc.tensor.matmul, nc.tensor.transpose

                def k_cols(b):
                    pe.wait_ge(ks_done, b.n + 1)
                    wait(pe, pv_done, 2 * b.n - 3)
                    for c in range(NC):
                        last = tr(p_pv[:, 128 * c:128 * c + 128], ks[:, 2 * c:2 * c + 2, :].rearrange("p g r -> p (g r)"), ident[:, :])
                    last.then_inc(k_mm, 1)

                def q_cols(b, c):
                    pe.wait_ge(qs_done, b.n + 1)
                    wait(pe, tq_done, 4 * b.n + c)
                    for i in range(G):
                        last = tr(p_tq[:, 128 * i:128 * i + 128], qs[b.par][:, c, i, :, :].rearrange("p g r -> p (g r)"), ident[:, :])
                    last.then_inc(tq_mm, 1)

                def pv(b, s):
                    pe.wait_ge(exp_done, 4 * b.n + 2 * s + 2)
                    if s == 0:
                        pe.wait_ge(v_in[b.par], 16 * (b.half + 1))
                    wait(pe, pv_done, 2 * b.n + s)
                    if s == 1 and (b + 2).ok:
                        pe.wait_ge(kt_done, b.n + 3)
                    if s == 0 and (b - 2).ok:
                        pe.wait_ge(xnT_done, b.n - 1)
                    for q in range(4):
                        g = 4 * s + q
                        last = mm(p_pv[32 * q:32 * q + 32, :], vals[b.par][:, g, :],
                                  probs[2 * s + q // 2][:, 512 * (q % 2):512 * (q % 2) + 512], start=True, stop=True)
                    last.then_inc(pv_mm, 1)

                def o_cols(b, s):
                    pe.wait_ge(pv_done, 2 * b.n + s + 1)
                    wait(pe, ot_done, 2 * b.n + s)
                    if s == 0 and (b - 3).ok:
                        pe.wait_ge(lg_done, b.n - 2)
                    for i in range(G):
                        last = tr(p_ot[:, 128 * i:128 * i + 128], ot_sb[s][:, 128 * i:128 * i + 128], ident[:, :])
                    last.then_inc(ot_mm, 1)

                def body(B):
                    if isinstance(B.n, int) and B.n == 0:
                        k_cols(B)
                        q_cols(B, 0)
                    for c in range(NC):
                        b = B - 1
                        if b.ok:
                            pe.wait_ge(mrow_in[c % 2], 32 * (2 * b.n + c // 2 + 1))
                            wait(pe, exp_done, 4 * b.n + c)
                            for g2 in range(2):
                                last = mm(p_exp[:, g2, :], kt[b.par][:, c, 128 * g2:128 * g2 + 128], qt[b.par][:, c, :],
                                          start=True, stop=True)
                            last.then_inc(p2_mm, 1)
                        if c == 1 and (B - 3).ok:
                            b = B - 3
                            pe.wait_ge(xn_done, b.n + 1)
                            pe.wait_ge(pv_done, 2 * b.n + (4 if (b + 1).ok else 2))
                            wait(pe, xnT_done, b.n)
                            for k in range(KC):
                                last = tr(p_pv[:, 128 * k:128 * k + 128], xn[b.par][:, 128 * k:128 * k + 128], ident[:, :])
                            last.then_inc(xnT_mm, 1)
                        if c == 3 and (B + 1).ok:
                            k_cols(B + 1)
                        if c == 2 and (B - 1).ok:
                            pv(B - 1, 0)
                        if c == 2 and (B - 4).ok:
                            b = B - 4
                            pe.wait_ge(xnT_done, b.n + 1)
                            pe.wait_ge(ot_done, 2 * b.n + 6 if (b + 2).ok else 2 * NB)
                            wait(pe, lg_done, b.n)
                            for k in range(KC):
                                last = mm(p_ot[:, 0:NE + 1], xnT[b.par][:, k, :], wr[:, k, :], start=(k == 0), stop=(k == KC - 1))
                            last.then_inc(lg_mm, 1)
                        if c == 0 and (B - 2).ok:
                            pv(B - 2, 1)
                        if c == 1 and (B - 2).ok:
                            o_cols(B - 2, 1)
                        if c == 3 and (B - 1).ok:
                            o_cols(B - 1, 0)
                        if c < 3 and B.ok:
                            q_cols(B, c + 1)
                        if c == 3 and (B + 1).ok:
                            q_cols(B + 1, 0)
                        if B.ok:
                            pe.wait_ge(tq_done, 4 * B.n + c + 1)
                            pe.wait_ge(kt_done, B.n + 1)
                            wait(pe, max_done, 4 * B.n + c)
                            for i in range(G):
                                last = mm(p_max[:, i // 2, 256 * (i % 2):256 * (i % 2) + 256], qt[B.par][:, c, 128 * i:128 * i + 128],
                                          kt[B.par][:, c, :], start=True, stop=True)
                            last.then_inc(p1_mm, 1)
                        b, cc = (B - 1, 3) if c == 0 else (B, c - 1)
                        if b.ok:
                            pe.wait_ge(max_done, 4 * b.n + cc + 1)
                            wait(pe, mt_done, 4 * b.n + cc)
                            last = tr(p_mt[:, :], negmax[cc % 2][:, :], ident[:, :])
                            last.then_inc(mt_mm, 1)
                iterations(pe, body)

        with ExitStack() as scope:
            sb, ps, sem = maker(scope)
            WORK = 2048
            chosen = sb("chosen", [128, NB, NE])
            eq = sb("eq", [128, NB, NE])
            iota_e = sb("iota_e", [128, NE])
            key_of = sb("key_of", [128, WORK])
            keys = sb("keys", [128, WORK])
            first = sb("first", [128, CAP])
            merge = sb("merge", [NE, 4 * CAP])
            firsts = sb("firsts", [NE, CAP])
            toks = sb("toks", [NE, CAP])
            halves = sb("halves", [CAP, 2, NPAIR])
            dv = sb("dv", [128, NB, TOPK])
            wsum, wrec = sb("wsum", [128, NB]), sb("wrec", [128, NB])
            route = sb("route", [128, NB, 2 * TOPK])
            zc, ez, ez1, sg = sb("zc", [128, NB]), sb("ez", [128, NB]), sb("ez1", [128, NB]), sb("sg", [128, NB])
            p_key = ps("p_key", [128, 4, 512])
            p_tok = ps("p_tok", [128, 512])
            chosen_done = sem("chosen_done")
            iota_done, key_mm, tok_mm, toks_done = sem("iota_done"), sem("key_mm"), sem("tok_mm"), sem("toks_done")
            dv_done, ew_done, route_done, route_out, seq = sem("dv_done"), sem("ew_done"), sem("route_done"), sem("route_out"), sem("r_seq")
            block = scope.enter_context(nc.Block())

            @block.gpsimd
            def _(pool):
                nc.gpsimd.iota(iota_e[:, :], pattern=[[1, NE]], base=0, channel_multiplier=0,
                               allow_small_or_imprecise_dtypes=True).then_inc(iota_done, 1)
                pool.wait_ge(iota_done, 1)
                for q in range(4):
                    nc.gpsimd.iota(key_of[32 * q:32 * q + 32, :], pattern=[[-4 * S, NB // 4], [-1, S]], base=TOK - S * q,
                                   channel_multiplier=0, allow_small_or_imprecise_dtypes=True).then_inc(iota_done, 1)

            @block.tensor
            def _(pe):
                pe.wait_ge(chosen_done, 1)
                for b in range(NB // 4):
                    last = nc.tensor.transpose(p_key[:, b // 4, 128 * (b % 4):128 * (b % 4) + 128],
                                               chosen[:, 4 * b:4 * b + 4, :].rearrange("p q e -> p (q e)"), ident[:, :])
                last.then_inc(key_mm, 1)
                pe.wait_ge(toks_done, 1)
                nc.tensor.transpose(p_tok[0:CAP, 0:NE], toks[:, :], ident[0:NE, 0:NE]).then_inc(tok_mm, 1)

            @block.scalar
            def _(act):
                act.wait_ge(dv_done, 1)
                nc.scalar.activation(route[:, :, TOPK:2 * TOPK], dv[:, :, :], ACT.Exp).then_inc(ew_done, 1)
                nc.scalar.activation(ez[:, :], zc[:, :], ACT.Exp, scale=-1.0).then_inc(ew_done, 1)

            @block.vector
            def _(dve):
                chain = Count(seq)

                def link(ins):
                    chain.inc(ins)
                    chain.wait(dve)

                dve.wait_ge(iota_done, 1)
                ti = top_idx[:, :].rearrange("p (b k) -> p b k", k=TOPK)
                for k in range(TOPK):
                    target = chosen if k == 0 else eq
                    link(nc.vector.tensor_tensor(target[:, :, :], iota_e[:, :].unsqueeze(1).to_broadcast([128, NB, NE]),
                                                 ti[:, :, k:k + 1].to_broadcast([128, NB, NE]), ALU.is_equal))
                    if k:
                        link(nc.vector.tensor_tensor(chosen[:, :, :], chosen[:, :, :], eq[:, :, :], ALU.add))
                dve.drain()
                dve.sem_inc(chosen_done, 1)
                nc.vector.tensor_scalar(zc[:, :], gate_z[:, :], -87.0, None, ALU.max)
                tv = top_val[:, :].rearrange("p (b k) -> p b k", k=TOPK)
                nc.vector.tensor_tensor(dv[:, :, :], tv, tv[:, :, 0:1].to_broadcast([128, NB, TOPK]), ALU.subtract).then_inc(dv_done, 1)
                nc.vector.tensor_copy(route[:, :, 0:TOPK], top_idx[:, :].rearrange("p (b k) -> p b k", k=TOPK))
                dve.wait_ge(ew_done, 2)
                link(nc.vector.tensor_reduce(wsum[:, :], route[:, :, TOPK:2 * TOPK], AX.X, ALU.add))
                link(nc.vector.reciprocal(wrec[:, :], wsum[:, :]))
                nc.vector.tensor_tensor(route[:, :, TOPK:2 * TOPK], route[:, :, TOPK:2 * TOPK],
                                        wrec[:, :].unsqueeze(2).to_broadcast([128, NB, TOPK]), ALU.mult).then_inc(route_done, 1)
                link(nc.vector.tensor_scalar(ez1[:, :], ez[:, :], 1.0, None, ALU.add))
                link(nc.vector.reciprocal(sg[:, :], ez1[:, :]))
                nc.vector.tensor_scalar(gate_s[:, :], sg[:, :], tanh_f[:, 0:1], None, ALU.mult)
                dve.wait_ge(iota_done, 5)
                dve.wait_ge(key_mm, 1)
                link(nc.vector.tensor_tensor(keys[:, :], p_key[:, :, :].rearrange("p a b -> p (a b)"), key_of[:, :], ALU.mult))
                for r in range(CAP // 8):
                    link(nc.vector.max(first[:, 8 * r:8 * r + 8], keys[:, :]))
                    if r < CAP // 8 - 1:
                        link(nc.vector.match_replace(keys[:, :], first[:, 8 * r:8 * r + 8], keys[:, :], 0.0))
                for q in range(4):
                    chain.inc(nc.vector.tensor_copy(merge[:, CAP * q:CAP * q + CAP], first[32 * q:32 * q + 32, :]))
                chain.wait(dve)
                for r in range(CAP // 8):
                    link(nc.vector.max(firsts[:, 8 * r:8 * r + 8], merge[:, :]))
                    if r < CAP // 8 - 1:
                        link(nc.vector.match_replace(merge[:, :], firsts[:, 8 * r:8 * r + 8], merge[:, :], 0.0))
                nc.vector.tensor_scalar(toks[:, :], firsts[:, :], -1.0, float(TOK), ALU.mult, ALU.add).then_inc(toks_done, 1)
                dve.wait_ge(tok_mm, 1)
                pt = p_tok[0:CAP, 0:NE].rearrange("c (i h) -> c h i", h=2)
                link(nc.vector.tensor_copy(halves[:, :, :], pt))
                nc.vector.tensor_copy(half_tok[:, :, :], halves[:, :, :])
                nc.vector.tensor_scalar(half_idx[:, :, :], halves[:, :, :], float(TOK - 1), None, ALU.min)
                nc.vector.tensor_scalar(half_used[:, :, :], halves[:, :, :], float(TOK), None, ALU.is_lt)
                for h in range(2):
                    nc.vector.tensor_scalar(slot_idx[CAP * h:CAP * h + CAP, :], halves[:, h, :], float(TOK - 1), None, ALU.min)

            @block.sync
            def _(sp):
                sp.wait_ge(route_done, 1)
                sp.dma_start(rw_dram.rearrange("(b t) c -> t b c", t=S), route[:, :, :]).then_inc(route_out, 16)
                sp.wait_ge(route_out, 16)

        routing.close()

        with ExitStack() as scope:
            sb, ps, sem = maker(scope)
            wgu_h = sb("wgu_h", [128, 2, KC, FS], F32R)
            wgu_l = sb("wgu_l", [128, 2, KC, FS], F32R)
            wd_h = sb("wd_h", [128, FC, E], F32R)
            wd_l = sb("wd_l", [128, FC, E], F32R)
            xraw = sb("xraw", [128, KC, TILE])
            xh = sb("xh", [128, KC, TILE], F32R)
            xl = sb("xl", [128, KC, TILE], F32R)
            act_f = sb("act_f", [128, TILE])
            hh = [sb(f"hh{i}", [128, TILE], F32R) for i in range(2)]
            hl = [sb(f"hl{i}", [128, TILE], F32R) for i in range(2)]
            rows = sb("rows", [128, TB, E])
            ew = sb("ew", [128, 2 * 2 * KC * FE])
            egu = ew[:, :].rearrange("p (h w k f) -> p h w k f", h=2, w=2, k=KC)
            edn = ew[:, 0:2 * 3 * E].rearrange("p (h c n) -> p h c n", h=2, c=3)
            xe = sb("xe", [128, E])
            xeT = sb("xeT", [128, KC, 128])
            eh = sb("eh", [128, FE])
            ehT = sb("ehT", [128, 3, 128])
            eo = sb("eo", [CAP, E])
            y1 = xe[0:CAP, :]
            cur_idx = sb("cur_idx", [128, 1], U32)
            cur_tok = [sb(f"cur_tok{h}", [CAP, 1], U32) for h in range(2)]
            cur_w = sb("cur_w", [CAP, 2])
            cur_g = sb("cur_g", [128, TB])
            rwg = sb("rwg", [CAP, NE, 2 * TOPK])
            gidx = [sb(f"gidx{i}", [CAP, 1], U32) for i in range(4)]
            e_of = sb("e_of", [CAP, NE])
            weq = ehT[0:CAP, 0, :].rearrange("p (e k) -> p e k", k=TOPK)
            w_slot = sb("w_slot", [CAP, 2, NPAIR])

            acc = ps("acc", [128, TB, 512])
            p_g, p_u = ps("p_g", [128, 512]), ps("p_u", [128, 512])
            p_x, p_y = ps("p_x", [128, 512]), ps("p_y", [128, 512])

            wraw_in = [sem(f"wraw_in{i}") for i in range(4)]
            whi_done, wlo_done = sem("whi_done"), sem("wlo_done")
            xraw_in, xhi_done, xlo_done = sem("xraw_in"), sem("xhi_done"), sem("xlo_done")
            g_mm, u_mm, dn_mm = sem("g_mm"), sem("u_mm"), sem("dn_mm")
            silu_done, h_done, hh_done, hl_done = sem("silu_done"), sem("h_done"), sem("hh_done"), sem("hl_done")
            rows_in, rows_out, add_done, gcur = sem("rows_in"), sem("rows_out"), sem("add_done"), sem("gcur")
            egu_in, edn_in = sem("egu_in"), sem("edn_in")
            xe_in, xeT_mm, xeT_done, eg_mm, eu_mm = sem("xe_in"), sem("xeT_mm"), sem("xeT_done"), sem("eg_mm"), sem("eu_mm")
            esilu_done, eh_done, ehT_mm, ehT_done, ed_mm = sem("esilu_done"), sem("eh_done"), sem("ehT_mm"), sem("ehT_done"), sem("ed_mm")
            eo_in, eo_out, eo_done, y_done = sem("eo_in"), sem("eo_out"), sem("eo_done"), sem("y_done")
            spare_p2, spare_s2 = sem("spare_p2"), sem("spare_s2")
            cur_set, wcur_set, eo_zero = sem("cur_set"), sem("wcur_set"), sem("eo_zero")
            rw_in = [sem(f"rw_in{i}") for i in range(4)]
            rw_set, eof_set, wchain = sem("rw_set"), sem("eof_set"), sem("wchain")

            SLOT = FS
            pieces = []
            for w, src in enumerate((Wsg, Wsu)):
                for k in range(KC):
                    pieces.append((src[128 * k:128 * k + 128, :], FS, wgu_h[:, w, k, :], wgu_l[:, w, k, :]))
            for f in range(0, FC, 2):
                n = min(2, FC - f)
                pieces.append((Wsd[128 * f:128 * (f + n), :].rearrange("(c p) n -> p c n", p=128), n * E,
                               wd_h[:, f:f + n, :].rearrange("p c n -> p (c n)"), wd_l[:, f:f + n, :].rearrange("p c n -> p (c n)")))
            NP = len(pieces)

            def staged(j):
                return ew[:, SLOT * (j % 4):SLOT * (j % 4) + pieces[j][1]]

            block = scope.enter_context(nc.Block())

            @block.sync
            def _(sp):
                def load_x(i):
                    sp.dma_start(xraw[:, :, :], xT_dram[:, :, bass.ts(i, TILE)].rearrange("k p t -> p k t")).then_inc(xraw_in, 16)

                def load_gate_up(i):
                    for h in range(2):
                        for w, src in enumerate((Wg, Wu)):
                            sp.dma_start(egu[:, h, w, :, :], src[2 * i + h].rearrange("(k p) f -> p k f", p=128)).then_inc(egu_in, 16)

                for j in range(NP):
                    wait(sp, wlo_done, j - 3)
                    n = pieces[j][1]
                    dst = staged(j) if n == FS else staged(j).rearrange("p (c n) -> p c n", n=E)
                    sp.dma_start(dst, pieces[j][0]).then_inc(wraw_in[j % 4], 16)
                    if j == 3:
                        load_x(0)
                sp.wait_ge(wlo_done, NP)
                load_gate_up(0)

                def body(i, last):
                    if not last:
                        sp.wait_ge(xlo_done, KC * i + KC)
                        load_x(i + 1)
                    sp.wait_ge(eu_mm, i + 1)
                    for h in range(2):
                        sp.dma_start(edn[:, h, 0:2, :], Wd[2 * i + h][0:256, :].rearrange("(c p) n -> p c n", p=128)).then_inc(edn_in, 16)
                        sp.dma_start(edn[0:FE - 256, h, 2, :], Wd[2 * i + h][256:FE, :]).then_inc(edn_in, 16)
                    sp.wait_ge(ed_mm, i + 1)
                    if not last:
                        load_gate_up(i + 1)
                    sp.wait_ge(eo_out, 32 * (i + 1))
                    sp.dma_start(rows[:, :, :], out_rows[bass.ts(i, TILE), :].rearrange("(j p) n -> p j n", p=128)).then_inc(rows_in, 16)
                    sp.wait_ge(add_done, TB * i + TB)
                    sp.dma_start(out_rows[bass.ts(i, TILE), :].rearrange("(j p) n -> p j n", p=128), rows[:, :, :]).then_inc(rows_out, 16)
                    sp.wait_ge(rows_out, 16 * (i + 1))
                    alone(sp, spare_s2)
                with sp.Fori(0, NT - 1) as i:
                    body(i, False)
                body(NT - 1, True)

            @block.gpsimd
            def _(pool):
                nc.gpsimd.memset(eo[:, :], 0.0).then_inc(eo_zero, 1)
                nc.gpsimd.iota(e_of[:, :], pattern=[[1, NE]], base=0, channel_multiplier=0,
                               allow_small_or_imprecise_dtypes=True).then_inc(eof_set, 1)
                for e in range(NE):
                    if e >= 4:
                        pool.wait_ge(rw_in[e % 4], 16 * (e // 4))
                    nc.gpsimd.tensor_copy(gidx[e % 4][:, :], half_idx[:, e % 2, e // 2:e // 2 + 1]).then_inc(rw_set, 1)
                    pool.wait_ge(rw_set, e + 1)
                    nc.gpsimd.indirect_dma_start(out=rwg[:, e, :], out_offset=None, in_=rw_dram,
                                                 in_offset=bass.IndirectOffsetOnAxis(ap=gidx[e % 4][:, 0:1], axis=0)).then_inc(rw_in[e % 4], 16)
                pool.wait_ge(eo_zero, 1)
                with pool.Fori(0, NT) as i:
                    pool.wait_ge(xeT_mm, i)
                    pool.wait_ge(eo_done, 2 * i)
                    alone(pool, spare_p2)
                    nc.gpsimd.tensor_copy(cur_idx[:, :], slot_idx[:, bass.ts(i, 1)])
                    for h in range(2):
                        last = nc.gpsimd.tensor_copy(cur_tok[h][:, :], half_tok[:, h, bass.ts(i, 1)])
                    last.then_inc(cur_set, 1)
                    pool.wait_ge(cur_set, i + 1)
                    alone(pool, spare_p2)
                    nc.gpsimd.indirect_dma_start(out=xe[:, :], out_offset=None, in_=xn_dram,
                                                 in_offset=bass.IndirectOffsetOnAxis(ap=cur_idx[:, 0:1], axis=0)).then_inc(xe_in, 16)
                    pool.wait_ge(rows_out, 16 * i)
                    alone(pool, spare_p2)
                    for h in range(2):
                        nc.gpsimd.indirect_dma_start(out=eo[:, :], out_offset=None, in_=out_rows,
                                                     in_offset=bass.IndirectOffsetOnAxis(ap=cur_tok[h][:, 0:1], axis=0),
                                                     bounds_check=TOK - 1, oob_is_err=False).then_inc(eo_in, 16)
                        pool.wait_ge(eo_done, 2 * i + h + 1)
                        alone(pool, spare_p2)
                        nc.gpsimd.indirect_dma_start(out=out_rows, out_offset=bass.IndirectOffsetOnAxis(ap=cur_tok[h][:, 0:1], axis=0),
                                                     in_=eo[:, :], in_offset=None,
                                                     bounds_check=TOK - 1, oob_is_err=False).then_inc(eo_out, 16)
                        pool.wait_ge(eo_out, 32 * i + 16 * h + 16)
                        alone(pool, spare_p2)

            @block.scalar
            def _(act):
                for j in range(NP):
                    act.wait_ge(wraw_in[j % 4], 16 * (j // 4 + 1))
                    nc.scalar.activation(pieces[j][2], staged(j), ACT.Copy).then_inc(whi_done, 1)

                def split_x(i):
                    act.wait_ge(xraw_in, 16 * (i + 1))
                    wait(act, u_mm, FC * i)
                    for k in range(KC):
                        nc.scalar.activation(xh[:, k, :], xraw[:, k, :], ACT.Copy).then_inc(xhi_done, 1)
                split_x(0)

                def body(i, last):
                    for f in range(FC):
                        act.wait_ge(g_mm, FC * i + f + 1)
                        wait(act, hl_done, FC * i + f)
                        nc.scalar.activation(act_f[:, :], p_g[:, :], ACT.Silu).then_inc(silu_done, 1)
                        if f == 0:
                            act.wait_ge(xeT_mm, i + 1)
                            nc.scalar.activation(xeT[:, :, :].rearrange("p k t -> p (k t)"), p_x[:, :], ACT.Copy).then_inc(xeT_done, 1)
                        if f == 1:
                            act.wait_ge(eg_mm, i + 1)
                            nc.scalar.activation(eh[:, :], p_y[:, 0:FE], ACT.Silu).then_inc(esilu_done, 1)
                        if f == 3:
                            act.wait_ge(ehT_mm, i + 1)
                            nc.scalar.activation(ehT[:, 0:2, :], p_y[:, 0:256].rearrange("p (c t) -> p c t", c=2), ACT.Copy)
                            nc.scalar.activation(ehT[0:FE - 256, 2, :], p_y[0:FE - 256, 256:384], ACT.Copy).then_inc(ehT_done, 1)
                    if not last:
                        split_x(i + 1)
                with act.Fori(0, NT - 1) as i:
                    body(i, False)
                body(NT - 1, True)

            @block.vector
            def _(dve):
                for j in range(NP):
                    dve.wait_ge(whi_done, j + 1)
                    nc.vector.tensor_tensor(pieces[j][3], staged(j), pieces[j][2].bitcast(F32), ALU.subtract).then_inc(wlo_done, 1)

                def split_x(i):
                    for k in range(KC):
                        dve.wait_ge(xhi_done, KC * i + k + 1)
                        nc.vector.tensor_tensor(xl[:, k, :], xraw[:, k, :], xh[:, k, :].bitcast(F32), ALU.subtract).then_inc(xlo_done, 1)
                split_x(0)
                for r in range(4):
                    dve.wait_ge(rw_in[r], 16 * (NE // 4))
                dve.wait_ge(eof_set, 1)
                chain = Count(wchain)

                def link(ins):
                    chain.inc(ins)
                    chain.wait(dve)
                link(nc.vector.tensor_tensor(weq[:, :, :], rwg[:, :, 0:TOPK], e_of[:, :].unsqueeze(2).to_broadcast([CAP, NE, TOPK]), ALU.is_equal))
                link(nc.vector.tensor_tensor(weq[:, :, :], weq[:, :, :], rwg[:, :, TOPK:2 * TOPK], ALU.mult))
                link(nc.vector.tensor_reduce(w_slot[:, :, :].rearrange("p h i -> p i h"), weq[:, :, :].rearrange("p (i h) k -> p i h k", h=2), AX.X, ALU.add))
                link(nc.vector.tensor_tensor(w_slot[:, :, :], w_slot[:, :, :], half_used[:, :, :], ALU.mult))
                link(nc.vector.tensor_scalar(w_slot[:, :, :], w_slot[:, :, :], tanh_f[0:CAP, 0:1], None, ALU.mult))

                def body(i, last):
                    for f in range(FC):
                        dve.wait_ge(silu_done, FC * i + f + 1)
                        dve.wait_ge(u_mm, FC * i + f + 1)
                        nc.vector.tensor_tensor(act_f[:, :], p_u[:, :], act_f[:, :], ALU.mult).then_inc(h_done, 1)
                        dve.wait_ge(h_done, FC * i + f + 1)
                        wait(dve, dn_mm, FC * i + max(f - 1, 0))
                        nc.vector.tensor_copy(hr(hh, f)[:, :], act_f[:, :]).then_inc(hh_done, 1)
                        dve.wait_ge(hh_done, FC * i + f + 1)
                        nc.vector.tensor_tensor(hr(hl, f)[:, :], act_f[:, :], hr(hh, f)[:, :].bitcast(F32), ALU.subtract).then_inc(hl_done, 1)
                        if f == 1:
                            dve.wait_ge(esilu_done, i + 1)
                            dve.wait_ge(eu_mm, i + 1)
                            nc.vector.tensor_tensor(eh[:, :], p_x[:, 0:FE], eh[:, :], ALU.mult).then_inc(eh_done, 1)
                        if f == 4:
                            nc.vector.tensor_copy(cur_w[:, :], w_slot[:, :, bass.ts(i, 1)].rearrange("p h a -> p (h a)"))
                            nc.vector.tensor_copy(cur_g[:, :], gate_s[:, bass.ts(i, TB)]).then_inc(wcur_set, 1)
                        if f == 5:
                            dve.wait_ge(wcur_set, i + 1)
                            dve.wait_ge(ed_mm, i + 1)
                            dve.wait_ge(eo_in, 32 * i + 16)
                            nc.vector.scalar_tensor_tensor(eo[:, :], p_x[0:CAP, :], cur_w[:, 0:1], eo[:, :], ALU.mult, ALU.add).then_inc(eo_done, 1)
                            nc.vector.tensor_copy(y1, p_x[CAP:2 * CAP, :]).then_inc(y_done, 1)
                        if f == 7:
                            dve.wait_ge(y_done, i + 1)
                            dve.wait_ge(eo_in, 32 * i + 32)
                            nc.vector.scalar_tensor_tensor(eo[:, :], y1, cur_w[:, 1:2], eo[:, :], ALU.mult, ALU.add).then_inc(eo_done, 1)
                    if not last:
                        split_x(i + 1)
                    dve.wait_ge(rows_in, 16 * (i + 1))
                    dve.wait_ge(dn_mm, FC * i + FC)
                    for j in range(TB):
                        nc.vector.scalar_tensor_tensor(rows[:, j, :], acc[:, j, :], cur_g[:, j:j + 1], rows[:, j, :],
                                                       ALU.mult, ALU.add).then_inc(add_done, 1)
                with dve.Fori(0, NT - 1) as i:
                    body(i, False)
                body(NT - 1, True)

            @block.tensor
            def _(pe):
                mm, tr = nc.tensor.matmul, nc.tensor.transpose

                def down(i, f):
                    pe.wait_ge(hl_done, FC * i + f + 1)
                    if f == 0:
                        pe.wait_ge(add_done, TB * i)
                    for j in range(TB):
                        t = slice(128 * j, 128 * j + 128)
                        a, b = hr(hh, f), hr(hl, f)
                        mm(acc[:, j, :], a[:, t], wd_h[:, f, :], start=(f == 0), stop=False)
                        mm(acc[:, j, :], a[:, t], wd_l[:, f, :], start=False, stop=False)
                        last = mm(acc[:, j, :], b[:, t], wd_h[:, f, :], start=False, stop=(f == FC - 1))
                    last.then_inc(dn_mm, 1)

                pe.wait_ge(wlo_done, NP)

                def body(i):
                    for f in range(FC):
                        cols = slice(128 * f, 128 * f + 128)
                        for w, bank, done, free in ((0, p_g, g_mm, silu_done), (1, p_u, u_mm, h_done)):
                            wait(pe, free, FC * i + f)
                            for k in range(KC):
                                if f == 0 and w == 0:
                                    pe.wait_ge(xlo_done, KC * i + k + 1)
                                mm(bank[:, :], wgu_h[:, w, k, cols], xh[:, k, :], start=(k == 0), stop=False)
                                mm(bank[:, :], wgu_h[:, w, k, cols], xl[:, k, :], start=False, stop=False)
                                last = mm(bank[:, :], wgu_l[:, w, k, cols], xh[:, k, :], start=False, stop=(k == KC - 1))
                            last.then_inc(done, 1)
                        if f == 0:
                            pe.wait_ge(xe_in, 16 * (i + 1))
                            wait(pe, y_done, i)
                            for k in range(KC):
                                last = tr(p_x[:, 128 * k:128 * k + 128], xe[:, 128 * k:128 * k + 128], ident[:, :])
                            last.then_inc(xeT_mm, 1)
                        if f == 1:
                            pe.wait_ge(xeT_done, i + 1)
                            pe.wait_ge(egu_in, 64 * (i + 1))
                            for w, bank, done in ((0, p_y, eg_mm), (1, p_x, eu_mm)):
                                for k in range(KC):
                                    for h in range(2):
                                        last = mm(bank[CAP * h:CAP * h + CAP, 0:FE], xeT[:, k, CAP * h:CAP * h + CAP], egu[:, h, w, k, :],
                                                  start=(k == 0), stop=(k == KC - 1))
                                last.then_inc(done, 1)
                        if f == 3:
                            pe.wait_ge(eh_done, i + 1)
                            for c, (a, n) in enumerate(FEC):
                                last = tr(p_y[0:n, 128 * c:128 * c + 128], eh[:, a:a + n], ident[:, :])
                            last.then_inc(ehT_mm, 1)
                        if f == 5:
                            pe.wait_ge(ehT_done, i + 1)
                            pe.wait_ge(edn_in, 64 * (i + 1))
                            for c, (a, n) in enumerate(FEC):
                                for h in range(2):
                                    last = mm(p_x[CAP * h:CAP * h + CAP, :], ehT[0:n, c, CAP * h:CAP * h + CAP], edn[0:n, h, c, :],
                                              start=(c == 0), stop=(c == len(FEC) - 1))
                            last.then_inc(ed_mm, 1)
                        if f > 0:
                            down(i, f - 1)
                    down(i, FC - 1)
                with pe.Fori(0, NT) as i:
                    body(i)


def hr(pair, f):
    return pair[f % 2]


_INS = ['x', 'ctx_512', 'g_xattn', 'g_ffn', 'L0_ffn_Wr', 'L0_ffn_Wg', 'L0_ffn_Wu', 'L0_ffn_Wd', 'L0_ffn_Wsg', 'L0_ffn_Wsu',
        'L0_ffn_Wsd', 'L0_ffn_Wse']
_OUTS = [((NB, S, E), 'float32')]


def kernel(**inputs):
    import numpy as _np
    import concourse.bacc as _bacc
    from concourse import mybir as _mybir
    from concourse.bass_utils import run_bass_kernel_spmd as _run

    nc = _bacc.Bacc("TRN2", target_bir_lowering=False, num_devices=1)
    arrays, args = {}, []
    for name in _INS:
        a = _np.ascontiguousarray(inputs[name])
        arrays[f"in_{name}_dram"] = a
        args.append(nc.dram_tensor(f"in_{name}_dram", a.shape, _mybir.dt.from_np(a.dtype), kind="ExternalInput").ap())
    for i, (shape, dtype) in enumerate(_OUTS):
        dt = _mybir.dt.from_np(_np.dtype(dtype))
        args.append(nc.dram_tensor(f"out_{i}_dram", shape, dt, kind="ExternalOutput").ap())
    build(nc, *args)
    r = _run(nc, [arrays], core_ids=[0])
    got = tuple(r.results[0][f"out_{i}_dram"] for i in range(len(_OUTS)))
    return got[0]
```

```python
import concourse.bass as bass
from concourse import mybir
from contextlib import ExitStack

F32 = mybir.dt.float32
F32R = mybir.dt.float32r
U32 = mybir.dt.uint32
I32 = mybir.dt.int32
ALU = mybir.AluOpType
ACT = mybir.ActivationFunctionType
AX = mybir.AxisListType

NB, S, E = 64, 128, 512
NH, NKV, D = 32, 8, 16
G = NH // NKV
KC = E // 128
TOK = NB * S
NE, TOPK, CAP = 32, 4, 64
FE, FS = 352, 1408
FC = FS // 128
EPS = 1e-5
NC = 4
ROW = E + 2 * TOPK
TILE = 512
NT = TOK // TILE
TB = TILE // S
NPAIR = NE // 2
FEC = [(0, 128), (128, 128), (256, FE - 256)]


def wait(eng, sem, value):
    if not isinstance(value, int) or value > 0:
        eng.wait_ge(sem, value)


def alone(eng, sem):
    eng.sem_inc(sem, 1)


class Count:

    def __init__(self, sem):
        self.sem, self.at, self.base, self.turn = sem, 0, 0, 0

    def inc(self, ins, n=1):
        self.at += n
        ins.then_inc(self.sem, n)

    def value(self):
        return self.base + self.at + self.turn

    def wait(self, eng):
        eng.wait_ge(self.sem, self.value())


class Batch:

    def __init__(self, pair, off):
        self.pair, self.off = pair, off

    def __add__(self, n):
        return Batch(self.pair, self.off + n)

    def __sub__(self, n):
        return Batch(self.pair, self.off - n)

    @property
    def n(self):
        return 2 * self.pair + self.off

    @property
    def half(self):
        return self.pair + self.off // 2

    @property
    def par(self):
        return self.off % 2

    @property
    def ok(self):
        return not isinstance(self.pair, int) or 0 <= self.n < NB


def build(nc, x, ctx_in, g_xattn, g_ffn, Wr, Wg, Wu, Wd, Wsg, Wsu, Wsd, Wse, out):
    x_t = x
    out_rows = out.rearrange("b s e -> (b s) e")
    xn_dram = nc.dram_tensor("xn_rows", (TOK + 1, ROW), F32, kind="Internal").ap()
    xT_dram = nc.dram_tensor("xn_cols", (KC, 128, TOK), F32, kind="Internal").ap()

    stack = ExitStack()
    with stack:
        def maker(scope):
            def sb(name, shape, dt=F32):
                return scope.enter_context(nc.sbuf_tensor(name, shape, dt))

            def ps(name, shape, dt=F32):
                return scope.enter_context(nc.psum_tensor(name, shape, dt))

            def sem(name):
                return scope.enter_context(nc.semaphore(name))
            return sb, ps, sem

        sb, _, sem = maker(stack)
        ident = sb("ident", [128, 128])
        tanh_x = sb("tanh_x", [128, 1])
        tanh_f = sb("tanh_f", [128, 1])
        slot_idx = sb("slot_idx", [128, NPAIR], U32)
        half_tok = sb("half_tok", [CAP, 2, NPAIR], U32)
        gate_s = sb("gate_s", [128, NB])
        top = sb("top", [128, 2, NB * TOPK])
        top_val, top_idx = top[:, 0, :], top[:, 1, :]
        gate_z = sb("gate_z", [128, NB])
        WORK = TOK // 4
        chosen = sb("chosen", [128, NB, NE])
        keys = sb("keys", [128, WORK])

        with ExitStack() as scope:
            sb, ps, sem = maker(scope)
            xs = [sb(f"xs{i}", [128, E]) for i in range(2)]
            xres = [sb(f"xres{i}", [128, E]) for i in range(2)]
            kv = [sb(f"kv{i}", [128, NKV * D]) for i in range(2)]
            vals = [sb(f"vals{i}", [128, NKV, 32]) for i in range(2)]
            ks = sb("ks", [128, NKV, 64])
            qraw = [sb(f"qraw{i}", [128, E]) for i in range(2)]
            qs = [sb(f"qs{i}", [128, NC, G, 2, 64]) for i in range(2)]
            qt = [sb(f"qt{i}", [128, NC, G * 128], F32R) for i in range(2)]
            kt = [sb(f"kt{i}", [128, NC, 2 * 128], F32R) for i in range(2)]
            probs = [sb(f"probs{i}", [128, 2 * 512]) for i in range(4)]
            ot_sb = [sb(f"ot_sb{i}", [128, 512]) for i in range(2)]
            o_sb = sb("o_sb", [128, E])
            rec = sb("rec", [128, 16])
            x2 = [sb(f"x2_{i}", [128, E]) for i in range(2)]
            xn = [sb(f"xn_{i}", [128, E]) for i in range(2)]
            xnT = [sb(f"xnT{i}", [128, KC, 128]) for i in range(2)]
            wr = sb("wr", [128, KC, NE + 1])
            negmax = [sb(f"negmax{i}", [128, 8]) for i in range(2)]
            mt = [sb(f"mt{i}", [8, 128], F32R) for i in range(2)]
            st1, st2 = sb("st1", [128, 6]), sb("st2", [128, 6])
            mv1 = [sb(f"mv1_{i}", [128, 2]) for i in range(2)]
            mv2 = [sb(f"mv2_{i}", [128, 2]) for i in range(2)]
            ve1, rs1 = sb("ve1", [128, 1]), sb("rs1", [128, 1])
            ve2, rs2 = sb("ve2", [128, 1]), sb("rs2", [128, 1])
            mhalf = sb("mhalf", [128, 1])
            lg = sb("lg", [128, NE + 1])
            v8 = sb("v8", [128, 8])
            i8 = sb("i8", [128, 8], U32)
            iota_e = sb("iota_e", [128, NE])
            idx_f = sb("idx_f", [128, TOPK])
            is_top = sb("is_top", [128, TOPK, NE])
            two_sum = sb("two_sum", [128, 2, NE])
            one_sum = sb("one_sum", [128, NE])
            gx, gf = sb("gx", [128, 1]), sb("gf", [128, 1])

            p_max = ps("p_max", [128, 2, 512])
            p_exp = ps("p_exp", [128, 2, 512])
            p_tq = ps("p_tq", [128, 512])
            p_pv = ps("p_pv", [128, 512])
            p_ot = ps("p_ot", [128, 512])
            p_mt = ps("p_mt", [8, 128])

            x_in = [sem(f"x_in{i}") for i in range(2)]
            kv_in = [sem(f"kv_in{i}") for i in range(2)]
            xres_in = [sem(f"xres_in{i}") for i in range(2)]
            v_in = [sem(f"v_in{i}") for i in range(2)]
            mrow_in = [sem(f"mrow_in{i}") for i in range(2)]
            x2_out = [sem(f"x2_out{i}") for i in range(2)]
            xn_out = [sem(f"xn_out{i}") for i in range(2)]
            xnT_out = [sem(f"xnT_out{i}") for i in range(2)]
            wr_in, g_in = sem("wr_in"), sem("g_in")
            spare_d, spare_p, spare_s = sem("spare_d"), sem("spare_p"), sem("spare_s")
            consts, tanh_done = sem("consts"), sem("tanh_done")
            pads, id0, keys_set = sem("pads"), sem("id0"), sem("keys_set")
            rs1_done, rs2_done, qraw_done = sem("rs1_done"), sem("rs2_done"), sem("qraw_done")
            top_done, kept = sem("top_done"), sem("kept")
            stat1, stat2 = sem("stat1"), sem("stat2")
            ks_done, qs_done, xn_done = sem("ks_done"), sem("qs_done"), sem("xn_done")
            pool_chain, dve_chain = sem("pool_chain"), sem("dve_chain")
            tq_mm, k_mm, p1_mm, p2_mm = sem("tq_mm"), sem("k_mm"), sem("p1_mm"), sem("p2_mm")
            pv_mm, ot_mm, mt_mm = sem("pv_mm"), sem("ot_mm"), sem("mt_mm")
            xnT_mm, lg_mm = sem("xnT_mm"), sem("lg_mm")
            max_done, exp_done, tq_done = sem("max_done"), sem("exp_done"), sem("tq_done")
            kt_done, pv_done, mt_done = sem("kt_done"), sem("pv_done"), sem("mt_done")
            ot_done, x2_done, xnT_done, lg_done = sem("ot_done"), sem("x2_done"), sem("xnT_done"), sem("lg_done")

            FIRST, LAST = 5, 61

            def iterations(eng, body, count=None):
                for b in range(FIRST):
                    body(Batch((b - 1) // 2, b - 2 * ((b - 1) // 2)))
                start = count.at if count else 0
                with eng.Fori((FIRST - 1) // 2, (LAST - 1) // 2) as pair:
                    if count:
                        count.turn = (pair - (FIRST - 1) // 2) * count.per_turn
                    body(Batch(pair, 1))
                    body(Batch(pair, 2))
                if count:
                    assert count.at - start == count.per_turn, count.at - start
                    count.turn = 0
                    count.at = start + count.per_turn * ((LAST - FIRST) // 2)
                for b in range(LAST, NB + 4):
                    body(Batch((b - 1) // 2, b - 2 * ((b - 1) // 2)))

            block = scope.enter_context(nc.Block())

            @block.sync
            def _(sp):
                sp.dma_start(wr[:, :, 0:NE], Wr.rearrange("(k p) e -> p k e", p=128)).then_inc(wr_in, 16)
                sp.dma_start(wr[:, :, NE:NE + 1], Wse.rearrange("(k p) e -> p k e", p=128),
                             allow_slow_non_contiguous=True).then_inc(wr_in, 16)
                sp.dma_start(gx[:, :], g_xattn.rearrange("(a n) -> a n", a=1).to_broadcast([128, 1])).then_inc(g_in, 16)
                sp.dma_start(gf[:, :], g_ffn.rearrange("(a n) -> a n", a=1).to_broadcast([128, 1])).then_inc(g_in, 16)

                def load_in(b):
                    wait(sp, qraw_done, b.n - 1)
                    sp.dma_start(xs[b.par][:, :], x_t[b.n]).then_inc(x_in[b.par], 16)
                    wait(sp, ks_done, b.n - 1)
                    sp.dma_start(kv[b.par][:, :], ctx_in[b.n]).then_inc(kv_in[b.par], 16)

                def body(B):
                    if isinstance(B.n, int) and B.n == 0:
                        load_in(B)
                        load_in(B + 1)
                        load_in(B + 2)
                    for c in range(NC):
                        m = (B - 1, 3) if c == 0 else (B, c - 1)
                        if m[0].ok:
                            b, cc = m
                            wait(sp, mt_done, 4 * b.n + cc + 1)
                            for g2 in range(2):
                                sp.dma_start(qt[b.par][64 * g2:64 * g2 + 1, cc, :].bitcast(F32),
                                             mt[cc % 2][4 * g2:4 * g2 + 4, :].bitcast(F32)).then_inc(mrow_in[cc % 2], 16)
                        if c == 0:
                            if (B - 1).ok:
                                wait(sp, x2_done, (B - 1).n - 1)
                                sp.dma_start(xres[(B - 1).par][:, :], x_t[(B - 1).n]).then_inc(xres_in[(B - 1).par], 16)
                            if (B - 3).ok:
                                b = B - 3
                                wait(sp, xn_done, b.n + 1)
                                sp.dma_start(xn_dram[bass.ts(b.n, 128), 0:E], xn[b.par][:, :]).then_inc(xn_out[b.par], 16)
                        if c == 1:
                            if (B + 3).ok:
                                load_in(B + 3)
                            if B.ok:
                                wait(sp, pv_mm, 2 * (B.n - 1))
                                if isinstance(B.n, int) and B.n < 2:
                                    sp.wait_ge(pads, 4)
                                sp.dma_start(vals[B.par][:, :, 0:D], ctx_in[B.n].rearrange("t (g d) -> t g d", d=D)).then_inc(v_in[B.par], 16)
                            if (B - 3).ok:
                                b = B - 3
                                wait(sp, xnT_done, b.n + 1)
                                alone(sp, spare_s)
                                sp.dma_start(xT_dram[:, :, bass.ts(b.n, 128)].rearrange("k p t -> p k t"), xnT[b.par][:, :, :]).then_inc(xnT_out[b.par], 16)
                        if c == 2 and (B - 2).ok:
                            b = B - 2
                            wait(sp, x2_done, b.n + 1)
                            sp.dma_start(out_rows[bass.ts(b.n, 128), :], x2[b.par][:, :]).then_inc(x2_out[b.par], 16)
                iterations(sp, body)
                for s in (x2_out, xn_out, xnT_out):
                    for i in range(2):
                        sp.wait_ge(s[i], 16 * (NB // 2))

            @block.gpsimd
            def _(pool):
                nc.gpsimd.memset(ident[:, :], 0.0).then_inc(id0, 1)
                pool.wait_ge(id0, 1)
                nc.gpsimd.affine_select(out=ident[:, :], in_=ident[:, :], compare_op=ALU.not_equal, fill=1.0, base=0,
                                        pattern=[[-1, 128]], channel_multiplier=1).then_inc(consts, 1)
                nc.gpsimd.memset(mhalf[:, :], -0.5).then_inc(id0, 1)
                pool.wait_ge(id0, 2)
                nc.gpsimd.iota(iota_e[:, :], pattern=[[1, NE]], base=0, channel_multiplier=0,
                               allow_small_or_imprecise_dtypes=True).then_inc(id0, 1)
                pool.wait_ge(id0, 3)
                pool.wait_ge(pads, 8)
                chain = Count(pool_chain)

                def inverse_root(b, stat, mv, ve, rs, used, done):
                    pool.wait_ge(stat, b.n + 1)
                    alone(pool, spare_p)
                    chain.inc(nc.gpsimd.tensor_scalar(ve[:, :], mv[b.par][:, 1:2], EPS, None, ALU.add))
                    chain.wait(pool)
                    wait(pool, used, b.n)
                    alone(pool, spare_p)
                    nc.gpsimd.tensor_tensor(rs[:, :], ve[:, :], mhalf[:, :], ALU.pow).then_inc(done, 1)

                def k_stacks(b):
                    pool.wait_ge(kv_in[b.par], 16 * (b.half + 1))
                    wait(pool, k_mm, b.n)
                    alone(pool, spare_p)
                    kin = kv[b.par][:, :].rearrange("p (g d) -> p g d", d=D)
                    nc.gpsimd.tensor_scalar(ks[:, :, 16:32].bitcast(F32R), kin, 1.0, 0.0, ALU.mult, ALU.add)
                    chain.inc(nc.gpsimd.tensor_scalar(ks[:, :, 48:64].bitcast(F32R), kin, 1.0, 0.0, ALU.mult, ALU.add))
                    chain.wait(pool)
                    nc.gpsimd.tensor_tensor(ks[:, :, 32:48], kin, ks[:, :, 16:32], ALU.subtract).then_inc(ks_done, 1)

                def q_stacks(b):
                    pool.wait_ge(qraw_done, b.n + 1)
                    wait(pool, tq_mm, 4 * (b.n - 1))
                    alone(pool, spare_p)

                    def stack(part, g2):
                        return qs[b.par][:, :, :, g2, 16 * part:16 * part + 16]

                    def heads(g2):
                        return qraw[b.par][:, :].rearrange("p (c g i d) -> p c g i d", g=2, i=G, d=D)[:, :, g2, :, :]

                    for part in (1, 2):
                        for g2 in range(2):
                            last = nc.gpsimd.tensor_scalar(stack(part, g2).bitcast(F32R), heads(g2), 1.0, 0.0, ALU.mult, ALU.add)
                    chain.inc(last)
                    chain.wait(pool)
                    for g2 in range(2):
                        last = nc.gpsimd.tensor_tensor(stack(3, g2), heads(g2), stack(1, g2), ALU.subtract)
                    last.then_inc(qs_done, 1)

                def body(B):
                    if isinstance(B.n, int) and B.n == 0:
                        inverse_root(B, stat1, mv1, ve1, rs1, qraw_done, rs1_done)
                        k_stacks(B)
                        q_stacks(B)
                        inverse_root(B + 1, stat1, mv1, ve1, rs1, qraw_done, rs1_done)
                    if (B + 1).ok:
                        k_stacks(B + 1)
                        q_stacks(B + 1)
                    if (B + 2).ok:
                        inverse_root(B + 2, stat1, mv1, ve1, rs1, qraw_done, rs1_done)
                    if (B - 2).ok:
                        inverse_root(B - 2, stat2, mv2, ve2, rs2, xn_done, rs2_done)
                    if isinstance(B.n, int) and 1 <= B.n <= 4:
                        q = B.n - 1
                        if q == 0:
                            pool.wait_ge(rs1_done, B.n + 3)
                        else:
                            pool.wait_ge(rs2_done, B.n - 1)
                        nc.gpsimd.iota(keys[32 * q:32 * q + 32, :], pattern=[[-4 * S, NB // 4], [-1, S]], base=TOK - S * q,
                                       channel_multiplier=0, allow_small_or_imprecise_dtypes=True).then_inc(keys_set, 1)
                        pool.wait_ge(keys_set, q + 1)
                    b = B - 4
                    if b.ok:
                        pool.wait_ge(top_done, b.n + 1)
                        alone(pool, spare_p)
                        nc.gpsimd.tensor_copy(top_val[:, bass.ts(b.n, TOPK)], v8[:, 0:TOPK])
                        nc.gpsimd.tensor_copy(gate_z[:, bass.ts(b.n, 1)], lg[:, NE:NE + 1])
                        nc.gpsimd.tensor_copy(top_idx[:, bass.ts(b.n, TOPK)], idx_f[:, :])
                        nc.gpsimd.tensor_tensor(two_sum[:, :, :], is_top[:, 0:2, :], is_top[:, 2:4, :], ALU.add).then_inc(kept, 1)
                        pool.wait_ge(kept, b.n + 1)
                        alone(pool, spare_p)
                        chain.inc(nc.gpsimd.tensor_tensor(one_sum[:, :], two_sum[:, 0, :], two_sum[:, 1, :], ALU.add))
                        chain.wait(pool)
                        alone(pool, spare_p)
                        nc.gpsimd.tensor_copy(chosen[:, bass.ts(b.n, 1), :].rearrange("p a e -> p (a e)"), one_sum[:, :])

                chain.per_turn = 2 * (1 + 1 + 1 + 1 + 1)
                iterations(pool, body, chain)

            @block.scalar
            def _(act):
                act.wait_ge(g_in, 32)
                nc.scalar.activation(tanh_x[:, :], gx[:, :], ACT.Tanh).then_inc(tanh_done, 1)
                nc.scalar.activation(tanh_f[:, :], gf[:, :], ACT.Tanh).then_inc(tanh_done, 1)
                act.wait_ge(pads, 8)

                def k_evac(b):
                    act.wait_ge(k_mm, b.n + 1)
                    wait(act, p2_mm, 4 * (b.n - 1))
                    nc.scalar.activation(kt[b.par][0:64, :, 0:128], p_pv[0:64, :].rearrange("p (c t) -> p c t", c=NC), ACT.Copy)
                    nc.scalar.activation(kt[b.par][64:128, :, 128:256], p_pv[64:128, :].rearrange("p (c t) -> p c t", c=NC),
                                         ACT.Copy).then_inc(kt_done, 1)

                def q_evac(b, c):
                    act.wait_ge(tq_mm, 4 * b.n + c + 1)
                    wait(act, p2_mm, 4 * (b.n - 2) + c + 1)
                    nc.scalar.activation(qt[b.par][:, c, :], p_tq[:, :], ACT.Copy).then_inc(tq_done, 1)

                def pv_evac(b, s):
                    act.wait_ge(pv_mm, 2 * b.n + s + 1)
                    wait(act, ot_mm, 2 * (b.n - 1) + s + 1)
                    nc.scalar.activation(ot_sb[s][:, :], p_pv[:, :], ACT.Copy).then_inc(pv_done, 1)

                def body(B):
                    if isinstance(B.n, int) and B.n == 0:
                        k_evac(B)
                        q_evac(B, 0)
                    for c in range(NC):
                        b = B - 1
                        if b.ok:
                            act.wait_ge(p2_mm, 4 * b.n + c + 1)
                            wait(act, pv_mm, 2 * (b.n - 1) + c // 2 + 1)
                            nc.scalar.activation(probs[c][:, :], p_exp[:, :, :].rearrange("p a b -> p (a b)"), ACT.Exp,
                                                 scale=float(D) ** -0.5).then_inc(exp_done, 1)
                        if c == 1 and (B - 3).ok:
                            b = B - 3
                            act.wait_ge(xnT_mm, b.n + 1)
                            wait(act, xnT_out[b.par], 16 * b.half)
                            wait(act, lg_mm, b.n - 1)
                            nc.scalar.activation(xnT[b.par][:, :, :].rearrange("p k t -> p (k t)"), p_pv[:, :], ACT.Copy).then_inc(xnT_done, 1)
                        if c == 0 and (B - 2).ok:
                            pv_evac(B - 2, 1)
                        if c == 2 and (B - 1).ok:
                            pv_evac(B - 1, 0)
                        if c == 3 and (B + 1).ok:
                            k_evac(B + 1)
                        if c < 3 and B.ok:
                            q_evac(B, c + 1)
                        if c == 3 and (B + 1).ok:
                            q_evac(B + 1, 0)
                        b, cc = (B - 1, 3) if c == 0 else (B, c - 1)
                        if b.ok:
                            act.wait_ge(mt_mm, 4 * b.n + cc + 1)
                            wait(act, mrow_in[cc % 2], 32 * (2 * b.n + cc // 2))
                            nc.scalar.activation(mt[cc % 2][:, :], p_mt[:, :], ACT.Copy).then_inc(mt_done, 1)
                iterations(act, body)

            @block.vector
            def _(dve):
                for i in range(2):
                    nc.vector.memset(vals[i][:, :, 16:32], 0.0).then_inc(pads, 1)
                dve.wait_ge(pads, 2)
                for i in range(2):
                    nc.vector.memset(vals[i][:, :, 16:17], 1.0).then_inc(pads, 1)
                for i in range(2):
                    nc.vector.memset(qs[i][:, :, :, :, 0:16], 0.0).then_inc(pads, 1)
                nc.vector.memset(kt[0][:, :, :].bitcast(F32), 0.0)
                nc.vector.memset(kt[1][:, :, :].bitcast(F32), 0.0).then_inc(pads, 1)
                nc.vector.memset(ks[:, :, 0:16], 0.0).then_inc(dve_chain, 1)
                chain = Count(dve_chain)
                chain.at = 1
                chain.wait(dve)
                nc.vector.memset(ks[:, :, 0:1], 1.0).then_inc(pads, 1)
                dve.wait_ge(id0, 3)
                dve.wait_ge(tanh_done, 2)

                def stats(source, st):
                    chain.inc(nc.vector.bn_stats(st[:, :], source))
                    return chain.value()

                def aggregate(b, st, count, mv, done):
                    dve.wait_ge(dve_chain, count)
                    alone(dve, spare_d)
                    nc.vector.bn_aggr(mv[b.par][:, :], st[:, :]).then_inc(done, 1)

                def stats_x(b):
                    dve.wait_ge(x_in[b.par], 16 * (b.half + 1))
                    return stats(xs[b.par][:, :], st1)

                def layer_norm(b, source, mv, rs, ready, target, done):
                    dve.wait_ge(ready, b.n + 1)
                    nc.vector.tensor_scalar(target[b.par][:, :], source[b.par][:, :], mv[b.par][:, 0:1], rs[:, 0:1],
                                            ALU.subtract, ALU.mult).then_inc(done, 1)

                def norm_x(b):
                    wait(dve, qs_done, b.n - 1)
                    layer_norm(b, xs, mv1, rs1, rs1_done, qraw, qraw_done)

                def p_out():
                    return p_ot[:, :].rearrange("p (i q r) -> p i q r", i=G, q=4)

                def invert_sums(b, s):
                    dve.wait_ge(ot_mm, 2 * b.n + s + 1)
                    chain.inc(nc.vector.reciprocal(rec[:, :].rearrange("p (i q) -> p i q", i=G), p_out()[:, :, :, D]))
                    return chain.value()

                def normalise(b, s, count):
                    dve.wait_ge(dve_chain, count)
                    if s == 0:
                        wait(dve, x2_done, b.n)
                    ov = o_sb[:, 256 * s:256 * s + 256].rearrange("p (q i d) -> p i q d", q=4, i=G)
                    rv = rec[:, :].rearrange("p (i q) -> p i q", i=G).unsqueeze(3).to_broadcast([128, G, 4, D])
                    nc.vector.tensor_tensor(ov, p_out()[:, :, :, 0:D], rv, ALU.mult).then_inc(ot_done, 1)

                def body(B):
                    if isinstance(B.n, int) and B.n == 0:
                        aggregate(B, st1, stats_x(B), mv1, stat1)
                        norm_x(B)
                        aggregate(B + 1, st1, stats_x(B + 1), mv1, stat1)
                    for c in range(NC):
                        if c == 2 and (B - 2).ok:
                            b = B - 2
                            dve.wait_ge(ot_done, 2 * b.n + 2)
                            dve.wait_ge(xres_in[b.par], 16 * (b.half + 1))
                            wait(dve, x2_out[b.par], 16 * b.half)
                            nc.vector.scalar_tensor_tensor(x2[b.par][:, :], o_sb[:, :], tanh_x[:, 0:1], xres[b.par][:, :],
                                                           ALU.mult, ALU.add).then_inc(x2_done, 1)
                        if c == 2 and (B - 4).ok:
                            b = B - 4
                            dve.wait_ge(lg_mm, b.n + 1)
                            wait(dve, kept, b.n)
                            nc.vector.tensor_copy(lg[:, :], p_ot[:, 0:NE + 1]).then_inc(lg_done, 1)
                        if c == 1:
                            if (B - 2).ok:
                                inverted = invert_sums(B - 2, 1)
                            if (B + 2).ok:
                                aggregate(B + 2, st1, x_stats, mv1, stat1)
                            if (B - 2).ok:
                                normalise(B - 2, 1, inverted)
                        if c == 2 and (B - 2).ok:
                            dve.wait_ge(x2_done, (B - 2).n + 1)
                            x2_stats = stats(x2[B.par][:, :], st2)
                        if B.ok:
                            dve.wait_ge(p1_mm, 4 * B.n + c + 1)
                            wait(dve, mt_mm, 4 * B.n + c - 1)
                            nc.vector.tensor_reduce(negmax[c % 2][:, :].rearrange("p (g i) -> p i g", i=G),
                                                    p_max[:, :, :].rearrange("p a (h g t) -> p (a h) g t", g=2, t=128),
                                                    AX.X, ALU.max, negate=True).then_inc(max_done, 1)
                        if c == 0:
                            if (B + 1).ok:
                                norm_x(B + 1)
                            if (B + 2).ok:
                                x_stats = stats_x(B + 2)
                        if c == 2 and (B - 4).ok:
                            dve.wait_ge(lg_done, (B - 4).n + 1)
                            alone(dve, spare_d)
                            chain.inc(nc.vector.max(v8[:, :], lg[:, 0:NE]))
                            top_count = chain.value()
                        if c == 2 and (B - 2).ok:
                            aggregate(B - 2, st2, x2_stats, mv2, stat2)
                        if c == 2 and (B - 4).ok:
                            dve.wait_ge(dve_chain, top_count)
                            alone(dve, spare_d)
                            chain.inc(nc.vector.max_index(i8[:, :], v8[:, :], lg[:, 0:NE]))
                            top_count = chain.value()
                        if c == 3 and (B - 4).ok:
                            dve.wait_ge(dve_chain, top_count)
                            alone(dve, spare_d)
                            chain.inc(nc.vector.tensor_copy(idx_f[:, :], i8[:, 0:TOPK]))
                            top_count = chain.value()
                        if c == 3 and (B - 1).ok:
                            normalise(B - 1, 0, invert_sums(B - 1, 0))
                        if c == 3 and (B - 2).ok:
                            b = B - 2
                            wait(dve, xnT_mm, b.n - 1)
                            wait(dve, xn_out[b.par], 16 * b.half)
                            layer_norm(b, x2, mv2, rs2, rs2_done, xn, xn_done)
                        if c == 3 and (B - 4).ok:
                            dve.wait_ge(dve_chain, top_count)
                            alone(dve, spare_d)
                            nc.vector.tensor_tensor(is_top[:, :, :], iota_e[:, :].unsqueeze(1).to_broadcast([128, TOPK, NE]),
                                                    idx_f[:, :].unsqueeze(2).to_broadcast([128, TOPK, NE]), ALU.is_equal).then_inc(top_done, 1)
                chain.per_turn = 2 * (1 + 1 + 1 + 1 + 1 + 2)
                iterations(dve, body, chain)

            @block.tensor
            def _(pe):
                pe.wait_ge(consts, 1)
                pe.wait_ge(wr_in, 32)
                pe.wait_ge(pads, 8)
                mm, tr = nc.tensor.matmul, nc.tensor.transpose

                def k_cols(b):
                    pe.wait_ge(ks_done, b.n + 1)
                    wait(pe, pv_done, 2 * b.n - 3)
                    for c in range(NC):
                        last = tr(p_pv[:, 128 * c:128 * c + 128], ks[:, 2 * c:2 * c + 2, :].rearrange("p g r -> p (g r)"), ident[:, :])
                    last.then_inc(k_mm, 1)

                def q_cols(b, c):
                    pe.wait_ge(qs_done, b.n + 1)
                    wait(pe, tq_done, 4 * b.n + c)
                    for i in range(G):
                        last = tr(p_tq[:, 128 * i:128 * i + 128], qs[b.par][:, c, i, :, :].rearrange("p g r -> p (g r)"), ident[:, :])
                    last.then_inc(tq_mm, 1)

                def pv(b, s):
                    pe.wait_ge(exp_done, 4 * b.n + 2 * s + 2)
                    if s == 0:
                        pe.wait_ge(v_in[b.par], 16 * (b.half + 1))
                    wait(pe, pv_done, 2 * b.n + s)
                    if s == 1 and (b + 2).ok:
                        pe.wait_ge(kt_done, b.n + 3)
                    if s == 0 and (b - 2).ok:
                        pe.wait_ge(xnT_done, b.n - 1)
                    for q in range(4):
                        g = 4 * s + q
                        last = mm(p_pv[32 * q:32 * q + 32, :], vals[b.par][:, g, :],
                                  probs[2 * s + q // 2][:, 512 * (q % 2):512 * (q % 2) + 512], start=True, stop=True)
                    last.then_inc(pv_mm, 1)

                def o_cols(b, s):
                    pe.wait_ge(pv_done, 2 * b.n + s + 1)
                    wait(pe, ot_done, 2 * b.n + s)
                    if s == 0 and (b - 3).ok:
                        pe.wait_ge(lg_done, b.n - 2)
                    for i in range(G):
                        last = tr(p_ot[:, 128 * i:128 * i + 128], ot_sb[s][:, 128 * i:128 * i + 128], ident[:, :])
                    last.then_inc(ot_mm, 1)

                def body(B):
                    if isinstance(B.n, int) and B.n == 0:
                        k_cols(B)
                        q_cols(B, 0)
                    for c in range(NC):
                        b = B - 1
                        if b.ok:
                            pe.wait_ge(mrow_in[c % 2], 32 * (2 * b.n + c // 2 + 1))
                            wait(pe, exp_done, 4 * b.n + c)
                            for g2 in range(2):
                                last = mm(p_exp[:, g2, :], kt[b.par][:, c, 128 * g2:128 * g2 + 128], qt[b.par][:, c, :],
                                          start=True, stop=True)
                            last.then_inc(p2_mm, 1)
                        if c == 1 and (B - 3).ok:
                            b = B - 3
                            pe.wait_ge(xn_done, b.n + 1)
                            pe.wait_ge(pv_done, 2 * b.n + (4 if (b + 1).ok else 2))
                            wait(pe, xnT_done, b.n)
                            for k in range(KC):
                                last = tr(p_pv[:, 128 * k:128 * k + 128], xn[b.par][:, 128 * k:128 * k + 128], ident[:, :])
                            last.then_inc(xnT_mm, 1)
                        if c == 3 and (B + 1).ok:
                            k_cols(B + 1)
                        if c == 2 and (B - 1).ok:
                            pv(B - 1, 0)
                        if c == 2 and (B - 4).ok:
                            b = B - 4
                            pe.wait_ge(xnT_done, b.n + 1)
                            pe.wait_ge(ot_done, 2 * b.n + 6 if (b + 2).ok else 2 * NB)
                            wait(pe, lg_done, b.n)
                            for k in range(KC):
                                last = mm(p_ot[:, 0:NE + 1], xnT[b.par][:, k, :], wr[:, k, :], start=(k == 0), stop=(k == KC - 1))
                            last.then_inc(lg_mm, 1)
                        if c == 0 and (B - 2).ok:
                            pv(B - 2, 1)
                        if c == 1 and (B - 2).ok:
                            o_cols(B - 2, 1)
                        if c == 3 and (B - 1).ok:
                            o_cols(B - 1, 0)
                        if c < 3 and B.ok:
                            q_cols(B, c + 1)
                        if c == 3 and (B + 1).ok:
                            q_cols(B + 1, 0)
                        if B.ok:
                            pe.wait_ge(tq_done, 4 * B.n + c + 1)
                            pe.wait_ge(kt_done, B.n + 1)
                            wait(pe, max_done, 4 * B.n + c)
                            for i in range(G):
                                last = mm(p_max[:, i // 2, 256 * (i % 2):256 * (i % 2) + 256], qt[B.par][:, c, 128 * i:128 * i + 128],
                                          kt[B.par][:, c, :], start=True, stop=True)
                            last.then_inc(p1_mm, 1)
                        b, cc = (B - 1, 3) if c == 0 else (B, c - 1)
                        if b.ok:
                            pe.wait_ge(max_done, 4 * b.n + cc + 1)
                            wait(pe, mt_done, 4 * b.n + cc)
                            last = tr(p_mt[:, :], negmax[cc % 2][:, :], ident[:, :])
                            last.then_inc(mt_mm, 1)
                iterations(pe, body)

        sb, _, sem = maker(stack)
        wgu_h = sb("wgu_h", [128, 2, KC, FS], F32R)
        wgu_l = sb("wgu_l", [128, 2, KC, FS], F32R)
        wd_h = sb("wd_h", [128, FC, E], F32R)
        wd_l = sb("wd_l", [128, FC, E], F32R)
        ew = sb("ew", [128, 2 * 2 * KC * FE])
        xh = sb("xh", [128, KC, TILE], F32R)
        xl = sb("xl", [128, KC, TILE], F32R)
        egu = ew[:, :].rearrange("p (h w k f) -> p h w k f", h=2, w=2, k=KC)
        egu_in = sem("egu_in")

        def load_gate_up(eng, i):
            for h in range(2):
                for w, src in enumerate((Wg, Wu)):
                    eng.dma_start(egu[:, h, w, :, :], src[2 * i + h].rearrange("(k p) f -> p k f", p=128)).then_inc(egu_in, 16)

        xraw = chosen[:, :, :].rearrange("p b e -> p (b e)").rearrange("p (k t) -> p k t", k=KC)
        xraw_in, xhi_done, xlo_done = sem("xraw_in"), sem("xhi_done"), sem("xlo_done")

        SLOT = FS
        pieces = []
        for w, src in enumerate((Wsg, Wsu)):
            for k in range(KC):
                pieces.append((src[128 * k:128 * k + 128, :], FS, wgu_h[:, w, k, :], wgu_l[:, w, k, :]))
        for f in range(0, FC, 2):
            n = min(2, FC - f)
            pieces.append((Wsd[128 * f:128 * (f + n), :].rearrange("(c p) n -> p c n", p=128), n * E,
                           wd_h[:, f:f + n, :].rearrange("p c n -> p (c n)"), wd_l[:, f:f + n, :].rearrange("p c n -> p (c n)")))
        NP = len(pieces)

        def staged(j):
            return ew[:, SLOT * (j % 4):SLOT * (j % 4) + pieces[j][1]]

        with ExitStack() as scope:
            sb, ps, sem = maker(scope)
            wraw_in = [sem(f"wraw_in{i}") for i in range(4)]
            whi_done, wlo_done = sem("whi_done"), sem("wlo_done")
            zeros = sb("zeros", [1, ROW])
            first = sb("first", [128, CAP])
            merge = sb("merge", [NE, 4 * CAP])
            firsts = sb("firsts", [NE, CAP])
            toks = sb("toks", [NE, CAP])
            halves = sb("halves", [CAP, 2, NPAIR])
            dv = sb("dv", [128, NB, TOPK])
            wsum, wrec = sb("wsum", [128, NB]), sb("wrec", [128, NB])
            route = sb("route", [128, NB, 2 * TOPK])
            zc, ez, ez1, sg = sb("zc", [128, NB]), sb("ez", [128, NB]), sb("ez1", [128, NB]), sb("sg", [128, NB])
            p_key = ps("p_key", [128, 4, 512])
            p_tok = ps("p_tok", [128, 512])
            zeros_set = sem("zeros_set")
            key_mm, tok_mm, toks_done = sem("key_mm"), sem("tok_mm"), sem("toks_done")
            dv_done, ew_done, route_done, route_out, seq = sem("dv_done"), sem("ew_done"), sem("route_done"), sem("route_out"), sem("r_seq")
            block = scope.enter_context(nc.Block())

            @block.gpsimd
            def _(pool):
                nc.gpsimd.memset(zeros[:, :], 0.0).then_inc(zeros_set, 1)
                pool.wait_ge(zeros_set, 1)
                for j in range(NP):
                    pool.wait_ge(whi_done, j + 1)
                    nc.gpsimd.tensor_tensor(pieces[j][3], staged(j), pieces[j][2].bitcast(F32), ALU.subtract).then_inc(wlo_done, 1)
                for k in range(KC):
                    pool.wait_ge(xhi_done, k + 1)
                    nc.gpsimd.tensor_tensor(xl[:, k, :], xraw[:, k, :], xh[:, k, :].bitcast(F32), ALU.subtract).then_inc(xlo_done, 1)

            @block.tensor
            def _(pe):
                for b in range(NB // 4):
                    last = nc.tensor.transpose(p_key[:, b // 4, 128 * (b % 4):128 * (b % 4) + 128],
                                               chosen[:, 4 * b:4 * b + 4, :].rearrange("p q e -> p (q e)"), ident[:, :])
                last.then_inc(key_mm, 1)
                pe.wait_ge(toks_done, 1)
                nc.tensor.transpose(p_tok[0:CAP, 0:NE], toks[:, :], ident[0:NE, 0:NE]).then_inc(tok_mm, 1)

            @block.scalar
            def _(act):
                for j in range(NP):
                    act.wait_ge(wraw_in[j % 4], 16 * (j // 4 + 1))
                    nc.scalar.activation(pieces[j][2], staged(j), ACT.Copy).then_inc(whi_done, 1)
                    if j == NP // 2:
                        act.wait_ge(dv_done, 1)
                        nc.scalar.activation(route[:, :, TOPK:2 * TOPK], dv[:, :, :], ACT.Exp).then_inc(ew_done, 1)
                        nc.scalar.activation(ez[:, :], zc[:, :], ACT.Exp, scale=-1.0).then_inc(ew_done, 1)
                act.wait_ge(xraw_in, 16)
                for k in range(KC):
                    nc.scalar.activation(xh[:, k, :], xraw[:, k, :], ACT.Copy).then_inc(xhi_done, 1)

            @block.vector
            def _(dve):
                chain = Count(seq)

                def link(ins):
                    chain.inc(ins)
                    chain.wait(dve)

                nc.vector.tensor_scalar(zc[:, :], gate_z[:, :], -87.0, None, ALU.max)
                tv = top_val.rearrange("p (b k) -> p b k", k=TOPK)
                nc.vector.tensor_tensor(dv[:, :, :], tv, tv[:, :, 0:1].to_broadcast([128, NB, TOPK]), ALU.subtract).then_inc(dv_done, 1)
                nc.vector.tensor_copy(route[:, :, 0:TOPK], top_idx.rearrange("p (b k) -> p b k", k=TOPK))
                dve.wait_ge(key_mm, 1)
                link(nc.vector.tensor_tensor(keys[:, :], p_key[:, :, :].rearrange("p a b -> p (a b)"), keys[:, :], ALU.mult))
                for r in range(CAP // 8):
                    link(nc.vector.max(first[:, 8 * r:8 * r + 8], keys[:, :]))
                    if r == 4:
                        dve.wait_ge(ew_done, 2)
                        link(nc.vector.tensor_reduce(wsum[:, :], route[:, :, TOPK:2 * TOPK], AX.X, ALU.add))
                        link(nc.vector.reciprocal(wrec[:, :], wsum[:, :]))
                        link(nc.vector.tensor_scalar(wrec[:, :], wrec[:, :], tanh_f[:, 0:1], None, ALU.mult))
                        nc.vector.tensor_tensor(route[:, :, TOPK:2 * TOPK], route[:, :, TOPK:2 * TOPK],
                                                wrec[:, :].unsqueeze(2).to_broadcast([128, NB, TOPK]), ALU.mult).then_inc(route_done, 1)
                        link(nc.vector.tensor_scalar(ez1[:, :], ez[:, :], 1.0, None, ALU.add))
                        link(nc.vector.reciprocal(sg[:, :], ez1[:, :]))
                        nc.vector.tensor_scalar(gate_s[:, :], sg[:, :], tanh_f[:, 0:1], None, ALU.mult)
                    if r < CAP // 8 - 1:
                        link(nc.vector.match_replace(keys[:, :], first[:, 8 * r:8 * r + 8], keys[:, :], 0.0))
                for q in range(4):
                    chain.inc(nc.vector.tensor_copy(merge[:, CAP * q:CAP * q + CAP], first[32 * q:32 * q + 32, :]))
                chain.wait(dve)
                for r in range(CAP // 8):
                    link(nc.vector.max(firsts[:, 8 * r:8 * r + 8], merge[:, :]))
                    if r < CAP // 8 - 1:
                        link(nc.vector.match_replace(merge[:, :], firsts[:, 8 * r:8 * r + 8], merge[:, :], 0.0))
                nc.vector.tensor_scalar(toks[:, :], firsts[:, :], -1.0, float(TOK), ALU.mult, ALU.add).then_inc(toks_done, 1)
                dve.wait_ge(tok_mm, 1)
                pt = p_tok[0:CAP, 0:NE].rearrange("c (i h) -> c h i", h=2)
                link(nc.vector.tensor_copy(halves[:, :, :], pt))
                nc.vector.tensor_copy(half_tok[:, :, :], halves[:, :, :])
                for h in range(2):
                    nc.vector.tensor_copy(slot_idx[CAP * h:CAP * h + CAP, :], halves[:, h, :])

            @block.sync
            def _(sp):
                for j in range(NP):
                    wait(sp, wlo_done, j - 3)
                    n = pieces[j][1]
                    dst = staged(j) if n == FS else staged(j).rearrange("p (c n) -> p c n", n=E)
                    sp.dma_start(dst, pieces[j][0]).then_inc(wraw_in[j % 4], 16)
                sp.wait_ge(key_mm, 1)
                sp.dma_start(xraw[:, :, :], xT_dram[:, :, 0:TILE].rearrange("k p t -> p k t")).then_inc(xraw_in, 16)
                sp.wait_ge(zeros_set, 1)
                sp.dma_start(xn_dram[TOK:TOK + 1, :], zeros[:, :]).then_inc(route_out, 16)
                sp.wait_ge(route_done, 1)
                sp.dma_start(xn_dram[0:TOK, E:ROW].rearrange("(b t) c -> t b c", t=S), route[:, :, :]).then_inc(route_out, 16)
                sp.wait_ge(wlo_done, NP)
                load_gate_up(sp, 0)
                sp.wait_ge(route_out, 32)


        with ExitStack() as scope:
            sb, ps, sem = maker(scope)
            act_f = sb("act_f", [128, TILE])
            hh = [sb(f"hh{i}", [128, TILE], F32R) for i in range(2)]
            hl = [sb(f"hl{i}", [128, TILE], F32R) for i in range(2)]
            rows = keys[:, :].rearrange("p (j n) -> p j n", j=TB)
            edn = ew[:, 0:2 * 3 * E].rearrange("p (h c n) -> p h c n", h=2, c=3)
            xe = sb("xe", [128, ROW])
            xeT = top[:, :, :].rearrange("p a n -> p (a n)").rearrange("p (k t) -> p k t", k=KC)
            eh = sb("eh", [128, FE])
            ehT = sb("ehT", [128, 3, 128])
            eo = sb("eo", [CAP, E])
            y1 = xe[0:CAP, 0:E]
            cur_idx = sb("cur_idx", [128, 1], U32)
            cur_tok = [sb(f"cur_tok{h}", [CAP, 1], U32) for h in range(2)]
            cur_w = sb("cur_w", [128, 1])
            cur_e = sb("cur_e", [128, 1])
            cur_g = sb("cur_g", [128, TB])
            e_of = sb("e_of", [128, NPAIR])
            weq = sb("weq", [128, TOPK])

            acc = ps("acc", [128, TB, 512])
            p_g, p_u = ps("p_g", [128, 512]), ps("p_u", [128, 512])
            p_x, p_y = ps("p_x", [128, 512]), ps("p_y", [128, 512])

            g_mm, u_mm, dn_mm = sem("g_mm"), sem("u_mm"), sem("dn_mm")
            silu_done, h_done, hh_done, hl_done = sem("silu_done"), sem("h_done"), sem("hh_done"), sem("hl_done")
            rows_in, rows_out, add_done = sem("rows_in"), sem("rows_out"), sem("add_done")
            edn_in = sem("edn_in")
            xe_in, xeT_mm, xeT_done, eg_mm, eu_mm = sem("xe_in"), sem("xeT_mm"), sem("xeT_done"), sem("eg_mm"), sem("eu_mm")
            esilu_done, eh_done, ehT_mm, ehT_done, ed_mm = sem("esilu_done"), sem("eh_done"), sem("ehT_mm"), sem("ehT_done"), sem("ed_mm")
            eo_in, eo_out, eo_done, y_done = sem("eo_in"), sem("eo_out"), sem("eo_done"), sem("y_done")
            spare_p2, spare_s2 = sem("spare_p2"), sem("spare_s2")
            cur_set, wcur_set, eo_zero = sem("cur_set"), sem("wcur_set"), sem("eo_zero")
            eof_set, weq_done, cur_w_set, cur_e_set = sem("eof_set"), sem("weq_done"), sem("cur_w_set"), sem("cur_e_set")

            block = scope.enter_context(nc.Block())

            @block.sync
            def _(sp):
                def load_x(i):
                    sp.dma_start(xraw[:, :, :], xT_dram[:, :, bass.ts(i, TILE)].rearrange("k p t -> p k t")).then_inc(xraw_in, 16)


                def body(i, last):
                    if not last:
                        sp.wait_ge(xlo_done, KC * i + KC)
                        load_x(i + 1)
                    sp.wait_ge(eu_mm, i + 1)
                    for h in range(2):
                        sp.dma_start(edn[:, h, 0:2, :], Wd[2 * i + h][0:256, :].rearrange("(c p) n -> p c n", p=128)).then_inc(edn_in, 16)
                        sp.dma_start(edn[0:FE - 256, h, 2, :], Wd[2 * i + h][256:FE, :]).then_inc(edn_in, 16)
                    sp.wait_ge(ed_mm, i + 1)
                    if not last:
                        load_gate_up(sp, i + 1)
                    sp.wait_ge(eo_out, 32 * (i + 1))
                    sp.dma_start(rows[:, :, :], out_rows[bass.ts(i, TILE), :].rearrange("(j p) n -> p j n", p=128)).then_inc(rows_in, 16)
                    sp.wait_ge(add_done, TB * i + TB)
                    sp.dma_start(out_rows[bass.ts(i, TILE), :].rearrange("(j p) n -> p j n", p=128), rows[:, :, :]).then_inc(rows_out, 16)
                    sp.wait_ge(rows_out, 16 * (i + 1))
                    alone(sp, spare_s2)
                with sp.Fori(0, NT - 1) as i:
                    body(i, False)
                body(NT - 1, True)

            @block.gpsimd
            def _(pool):
                nc.gpsimd.memset(eo[:, :], 0.0).then_inc(eo_zero, 1)
                for h in range(2):
                    if h == 0:
                        pool.wait_ge(eo_zero, 1)
                    else:
                        pool.wait_ge(eof_set, 1)
                    nc.gpsimd.iota(e_of[CAP * h:CAP * h + CAP, :], pattern=[[2, NPAIR]], base=h, channel_multiplier=0,
                                   allow_small_or_imprecise_dtypes=True).then_inc(eof_set, 1)
                pool.wait_ge(eof_set, 2)
                with pool.Fori(0, NT) as i:
                    pool.wait_ge(xeT_mm, i)
                    pool.wait_ge(eo_done, 2 * i)
                    alone(pool, spare_p2)
                    nc.gpsimd.tensor_copy(cur_idx[:, :], slot_idx[:, bass.ts(i, 1)])
                    for h in range(2):
                        last = nc.gpsimd.tensor_copy(cur_tok[h][:, :], half_tok[:, h, bass.ts(i, 1)])
                    last.then_inc(cur_set, 1)
                    pool.wait_ge(cur_set, i + 1)
                    alone(pool, spare_p2)
                    nc.gpsimd.indirect_dma_start(out=xe[:, :], out_offset=None, in_=xn_dram,
                                                 in_offset=bass.IndirectOffsetOnAxis(ap=cur_idx[:, 0:1], axis=0)).then_inc(xe_in, 16)
                    pool.wait_ge(rows_out, 16 * i)
                    alone(pool, spare_p2)
                    for h in range(2):
                        nc.gpsimd.indirect_dma_start(out=eo[:, :], out_offset=None, in_=out_rows,
                                                     in_offset=bass.IndirectOffsetOnAxis(ap=cur_tok[h][:, 0:1], axis=0),
                                                     bounds_check=TOK - 1, oob_is_err=False).then_inc(eo_in, 16)
                        pool.wait_ge(eo_done, 2 * i + h + 1)
                        alone(pool, spare_p2)
                        nc.gpsimd.indirect_dma_start(out=out_rows, out_offset=bass.IndirectOffsetOnAxis(ap=cur_tok[h][:, 0:1], axis=0),
                                                     in_=eo[:, :], in_offset=None,
                                                     bounds_check=TOK - 1, oob_is_err=False).then_inc(eo_out, 16)
                        pool.wait_ge(eo_out, 32 * i + 16 * h + 16)
                        alone(pool, spare_p2)

            @block.scalar
            def _(act):
                def split_x(i):
                    act.wait_ge(xraw_in, 16 * (i + 1))
                    wait(act, u_mm, FC * i)
                    for k in range(KC):
                        nc.scalar.activation(xh[:, k, :], xraw[:, k, :], ACT.Copy).then_inc(xhi_done, 1)

                def body(i, last):
                    for f in range(FC):
                        act.wait_ge(g_mm, FC * i + f + 1)
                        wait(act, hl_done, FC * i + f)
                        nc.scalar.activation(act_f[:, :], p_g[:, :], ACT.Silu).then_inc(silu_done, 1)
                        if f == 0:
                            act.wait_ge(xeT_mm, i + 1)
                            nc.scalar.activation(xeT[:, :, :].rearrange("p k t -> p (k t)"), p_x[:, :], ACT.Copy).then_inc(xeT_done, 1)
                        if f == 1:
                            act.wait_ge(eg_mm, i + 1)
                            nc.scalar.activation(eh[:, :], p_y[:, 0:FE], ACT.Silu).then_inc(esilu_done, 1)
                        if f == 3:
                            act.wait_ge(ehT_mm, i + 1)
                            nc.scalar.activation(ehT[:, 0:2, :], p_y[:, 0:256].rearrange("p (c t) -> p c t", c=2), ACT.Copy)
                            nc.scalar.activation(ehT[0:FE - 256, 2, :], p_y[0:FE - 256, 256:384], ACT.Copy).then_inc(ehT_done, 1)
                    if not last:
                        split_x(i + 1)
                with act.Fori(0, NT - 1) as i:
                    body(i, False)
                body(NT - 1, True)

            @block.vector
            def _(dve):
                def split_x(i):
                    for k in range(KC):
                        dve.wait_ge(xhi_done, KC * i + k + 1)
                        nc.vector.tensor_tensor(xl[:, k, :], xraw[:, k, :], xh[:, k, :].bitcast(F32), ALU.subtract).then_inc(xlo_done, 1)
                dve.wait_ge(eof_set, 2)

                def body(i, last):
                    for f in range(FC):
                        dve.wait_ge(silu_done, FC * i + f + 1)
                        dve.wait_ge(u_mm, FC * i + f + 1)
                        nc.vector.tensor_tensor(act_f[:, :], p_u[:, :], act_f[:, :], ALU.mult).then_inc(h_done, 1)
                        dve.wait_ge(h_done, FC * i + f + 1)
                        wait(dve, dn_mm, FC * i + max(f - 1, 0))
                        nc.vector.tensor_copy(hr(hh, f)[:, :], act_f[:, :]).then_inc(hh_done, 1)
                        dve.wait_ge(hh_done, FC * i + f + 1)
                        nc.vector.tensor_tensor(hr(hl, f)[:, :], act_f[:, :], hr(hh, f)[:, :].bitcast(F32), ALU.subtract).then_inc(hl_done, 1)
                        if f == 3:
                            nc.vector.tensor_copy(cur_e[:, :], e_of[:, bass.ts(i, 1)]).then_inc(cur_e_set, 1)
                            dve.wait_ge(cur_e_set, i + 1)
                        if f == 1:
                            dve.wait_ge(esilu_done, i + 1)
                            dve.wait_ge(eu_mm, i + 1)
                            nc.vector.tensor_tensor(eh[:, :], p_x[:, 0:FE], eh[:, :], ALU.mult).then_inc(eh_done, 1)
                        if f == 4:
                            dve.wait_ge(xe_in, 16 * (i + 1))
                            nc.vector.tensor_scalar(weq[:, :], xe[:, E:E + TOPK], cur_e[:, 0:1], None, ALU.is_equal).then_inc(weq_done, 1)
                            dve.wait_ge(weq_done, 2 * i + 1)
                            nc.vector.tensor_tensor(weq[:, :], weq[:, :], xe[:, E + TOPK:ROW], ALU.mult).then_inc(weq_done, 1)
                            dve.wait_ge(weq_done, 2 * i + 2)
                            nc.vector.tensor_reduce(cur_w[:, :], weq[:, :], AX.X, ALU.add).then_inc(cur_w_set, 1)
                            nc.vector.tensor_copy(cur_g[:, :], gate_s[:, bass.ts(i, TB)]).then_inc(wcur_set, 1)
                        if f == 5:
                            dve.wait_ge(cur_w_set, i + 1)
                            dve.wait_ge(ed_mm, i + 1)
                            dve.wait_ge(eo_in, 32 * i + 16)
                            nc.vector.scalar_tensor_tensor(eo[:, :], p_x[0:CAP, :], cur_w[0:CAP, 0:1], eo[:, :], ALU.mult, ALU.add).then_inc(eo_done, 1)
                            nc.vector.tensor_scalar(y1, p_x[CAP:2 * CAP, :], cur_w[CAP:2 * CAP, 0:1], None, ALU.mult).then_inc(y_done, 1)
                        if f == 7:
                            dve.wait_ge(y_done, i + 1)
                            dve.wait_ge(eo_in, 32 * i + 32)
                            nc.vector.tensor_tensor(eo[:, :], y1, eo[:, :], ALU.add).then_inc(eo_done, 1)
                    if not last:
                        split_x(i + 1)
                    dve.wait_ge(rows_in, 16 * (i + 1))
                    dve.wait_ge(wcur_set, i + 1)
                    dve.wait_ge(dn_mm, FC * i + FC)
                    for j in range(TB):
                        nc.vector.scalar_tensor_tensor(rows[:, j, :], acc[:, j, :], cur_g[:, j:j + 1], rows[:, j, :],
                                                       ALU.mult, ALU.add).then_inc(add_done, 1)
                with dve.Fori(0, NT - 1) as i:
                    body(i, False)
                body(NT - 1, True)

            @block.tensor
            def _(pe):
                mm, tr = nc.tensor.matmul, nc.tensor.transpose

                def down(i, f):
                    pe.wait_ge(hl_done, FC * i + f + 1)
                    if f == 0:
                        pe.wait_ge(add_done, TB * i)
                    for j in range(TB):
                        t = slice(128 * j, 128 * j + 128)
                        a, b = hr(hh, f), hr(hl, f)
                        mm(acc[:, j, :], a[:, t], wd_h[:, f, :], start=(f == 0), stop=False)
                        mm(acc[:, j, :], a[:, t], wd_l[:, f, :], start=False, stop=False)
                        last = mm(acc[:, j, :], b[:, t], wd_h[:, f, :], start=False, stop=(f == FC - 1))
                    last.then_inc(dn_mm, 1)

                def body(i):
                    for f in range(FC):
                        cols = slice(128 * f, 128 * f + 128)
                        for w, bank, done, free in ((0, p_g, g_mm, silu_done), (1, p_u, u_mm, h_done)):
                            wait(pe, free, FC * i + f)
                            for k in range(KC):
                                if f == 0 and w == 0:
                                    pe.wait_ge(xlo_done, KC * i + k + 1)
                                mm(bank[:, :], wgu_h[:, w, k, cols], xh[:, k, :], start=(k == 0), stop=False)
                                mm(bank[:, :], wgu_h[:, w, k, cols], xl[:, k, :], start=False, stop=False)
                                last = mm(bank[:, :], wgu_l[:, w, k, cols], xh[:, k, :], start=False, stop=(k == KC - 1))
                            last.then_inc(done, 1)
                        if f == 0:
                            pe.wait_ge(xe_in, 16 * (i + 1))
                            wait(pe, y_done, i)
                            for k in range(KC):
                                last = tr(p_x[:, 128 * k:128 * k + 128], xe[:, 128 * k:128 * k + 128], ident[:, :])
                            last.then_inc(xeT_mm, 1)
                        if f == 1:
                            pe.wait_ge(xeT_done, i + 1)
                            pe.wait_ge(egu_in, 64 * (i + 1))
                            for w, bank, done in ((0, p_y, eg_mm), (1, p_x, eu_mm)):
                                for k in range(KC):
                                    for h in range(2):
                                        last = mm(bank[CAP * h:CAP * h + CAP, 0:FE], xeT[:, k, CAP * h:CAP * h + CAP], egu[:, h, w, k, :],
                                                  start=(k == 0), stop=(k == KC - 1))
                                last.then_inc(done, 1)
                        if f == 3:
                            pe.wait_ge(eh_done, i + 1)
                            for c, (a, n) in enumerate(FEC):
                                last = tr(p_y[0:n, 128 * c:128 * c + 128], eh[:, a:a + n], ident[:, :])
                            last.then_inc(ehT_mm, 1)
                        if f == 5:
                            pe.wait_ge(ehT_done, i + 1)
                            pe.wait_ge(edn_in, 64 * (i + 1))
                            for c, (a, n) in enumerate(FEC):
                                for h in range(2):
                                    last = mm(p_x[CAP * h:CAP * h + CAP, :], ehT[0:n, c, CAP * h:CAP * h + CAP], edn[0:n, h, c, :],
                                              start=(c == 0), stop=(c == len(FEC) - 1))
                            last.then_inc(ed_mm, 1)
                        if f > 0:
                            down(i, f - 1)
                    down(i, FC - 1)
                with pe.Fori(0, NT) as i:
                    body(i)


def hr(pair, f):
    return pair[f % 2]


_INS = ['x', 'ctx_512', 'g_xattn', 'g_ffn', 'L0_ffn_Wr', 'L0_ffn_Wg', 'L0_ffn_Wu', 'L0_ffn_Wd', 'L0_ffn_Wsg', 'L0_ffn_Wsu',
        'L0_ffn_Wsd', 'L0_ffn_Wse']
_OUTS = [((NB, S, E), 'float32')]


def kernel(**inputs):
    import numpy as _np
    import concourse.bacc as _bacc
    from concourse import mybir as _mybir
    from concourse.bass_utils import run_bass_kernel_spmd as _run

    nc = _bacc.Bacc("TRN2", target_bir_lowering=False, num_devices=1)
    arrays, args = {}, []
    for name in _INS:
        a = _np.ascontiguousarray(inputs[name])
        arrays[f"in_{name}_dram"] = a
        args.append(nc.dram_tensor(f"in_{name}_dram", a.shape, _mybir.dt.from_np(a.dtype), kind="ExternalInput").ap())
    for i, (shape, dtype) in enumerate(_OUTS):
        dt = _mybir.dt.from_np(_np.dtype(dtype))
        args.append(nc.dram_tensor(f"out_{i}_dram", shape, dt, kind="ExternalOutput").ap())
    build(nc, *args)
    r = _run(nc, [arrays], core_ids=[0])
    got = tuple(r.results[0][f"out_{i}_dram"] for i in range(len(_OUTS)))
    return got[0]
```
